# Optimizing a Trainium2 kernel written in Bass

```python
import numpy as np
import jax
import jax.numpy as jnp

def _softmax(x, axis=-1):
    return jax.nn.softmax(x, axis=axis)

def _gelu(x):
    return jax.nn.gelu(x, approximate=True)

def _silu(x):
    return jax.nn.silu(x)

def _sigmoid(x):
    return jax.nn.sigmoid(x)

def _layernorm(x, axis=-1, eps=1e-05):
    m = jnp.mean(x, axis=axis, keepdims=True)
    v = jnp.var(x, axis=axis, keepdims=True)
    return (x - m) / jnp.sqrt(v + eps)

def _scatter_add(tgt, idx, src, axis=0):
    return tgt.at[idx].add(src)

def _segment_sum(src, seg, n):
    return jax.ops.segment_sum(src, seg, n)
kernel_name = 'mk_macaron_d2_jaxref_r8_1598c6'

def setup_inputs(seed: int=0):
    np.random.seed(seed)
    _w = jnp.asarray

    def _L0_attn_setup():
        import jax, jax.numpy as jnp
        import numpy as np
        B, S, D = (2, 256, 512)
        NH, NKV = (32, 8)
        HD = D // NH
        NREP = NH // NKV
        SCALE = HD ** (-0.5)
        key = jax.random.key(seed)
        kx, kq, kk, kv, ko = jax.random.split(key, 5)
        s = 0.02
        return {'x': jax.random.normal(kx, (B, S, D), dtype=jnp.float32), 'wq': jax.random.normal(kq, (D, NH * HD), dtype=jnp.float32) * s, 'wk': jax.random.normal(kk, (D, NKV * HD), dtype=jnp.float32) * s, 'wv': jax.random.normal(kv, (D, NKV * HD), dtype=jnp.float32) * s, 'wo': jax.random.normal(ko, (NH * HD, D), dtype=jnp.float32) * s}
    _L0_attn_in = _L0_attn_setup()

    def _L0_ffn_setup():
        import jax, jax.numpy as jnp
        import numpy as np
        HIDDEN = 512
        INTER = 1376
        BATCH, SEQ = (2, 256)
        key = jax.random.key(seed)
        ks = jax.random.split(key, 7)
        s_h = 1.0 / np.sqrt(HIDDEN)
        s_i = 1.0 / np.sqrt(INTER)
        return {'hidden_states': jax.random.normal(ks[0], (BATCH, SEQ, HIDDEN), dtype=jnp.float32), 'w_gate': jax.random.uniform(ks[1], (INTER, HIDDEN), jnp.float32, -s_h, s_h), 'b_gate': jax.random.uniform(ks[2], (INTER,), jnp.float32, -s_h, s_h), 'w_up': jax.random.uniform(ks[3], (INTER, HIDDEN), jnp.float32, -s_h, s_h), 'b_up': jax.random.uniform(ks[4], (INTER,), jnp.float32, -s_h, s_h), 'w_down': jax.random.uniform(ks[5], (HIDDEN, INTER), jnp.float32, -s_i, s_i), 'b_down': jax.random.uniform(ks[6], (HIDDEN,), jnp.float32, -s_i, s_i)}
    _L0_ffn_in = _L0_ffn_setup()

    def _L1_attn_setup():
        import jax, jax.numpy as jnp
        import numpy as np
        H, KV, HD, HID = (32, 8, 128, 512)
        THETA, FACTOR, HI_FF, LO_FF, ORIG_MAX = (500000.0, 8.0, 4.0, 1.0, 1024)

        def _llama3_inv_freq():
            inv = 1.0 / THETA ** (np.arange(0, HD, 2, dtype=np.float64) / HD)
            wavelen = 2.0 * np.pi / inv
            low_wl = ORIG_MAX / LO_FF
            high_wl = ORIG_MAX / HI_FF
            smooth = (ORIG_MAX / wavelen - LO_FF) / (HI_FF - LO_FF)
            scaled = np.where(wavelen > low_wl, inv / FACTOR, inv)
            mid = (wavelen <= low_wl) & (wavelen >= high_wl)
            scaled = np.where(mid, (1 - smooth) * inv / FACTOR + smooth * inv, scaled)
            return scaled.astype(np.float32)

        def _rope_cos_sin(T):
            inv = _llama3_inv_freq()
            pos = np.arange(T, dtype=np.float32)
            freqs = pos[:, None] * inv[None, :]
            emb = np.concatenate([freqs, freqs], axis=-1)
            return (jnp.asarray(np.cos(emb)), jnp.asarray(np.sin(emb)))

        def _rotate_half(x):
            x1, x2 = jnp.split(x, 2, axis=-1)
            return jnp.concatenate([-x2, x1], axis=-1)
        key = jax.random.key(seed)
        ks = jax.random.split(key, 5)
        s = 1.0 / np.sqrt(HID)
        return {'x': jax.random.normal(ks[0], (1, 256, HID), jnp.float32), 'wq': jax.random.normal(ks[1], (HID, H * HD), jnp.float32) * s, 'wk': jax.random.normal(ks[2], (HID, KV * HD), jnp.float32) * s, 'wv': jax.random.normal(ks[3], (HID, KV * HD), jnp.float32) * s, 'wo': jax.random.normal(ks[4], (H * HD, HID), jnp.float32) * s}
    _L1_attn_in = _L1_attn_setup()

    def _L1_ffn_setup():
        import jax, jax.numpy as jnp
        import numpy as np
        IN_FEATURES = 512

        def _dequantize(qweight, scale, zero_point):
            N, K_packed = qweight.shape
            groups = K_packed // 3
            p = qweight.reshape(N, groups, 3)
            v0 = p[:, :, 0] & 63
            v1 = p[:, :, 0] >> 6 & 63
            v2 = p[:, :, 1] & 63
            v3 = p[:, :, 2] & 63
            unpacked = jnp.stack([v0, v1, v2, v3], axis=2).reshape(N, groups * 4)
            unpacked = unpacked[:, :IN_FEATURES]
            return (unpacked.astype(jnp.float32) - zero_point) * scale
        key = jax.random.key(seed)
        k1, k2, k3, k4, k5 = jax.random.split(key, 5)
        x = jax.random.normal(k1, (8, 256, 512), dtype=jnp.float32)
        qweight = jax.random.randint(k2, (512, 384), 0, 512, dtype=jnp.int32)
        weight_scale = jax.random.uniform(k3, (512, 1), dtype=jnp.float32) * 0.02 + 0.001
        weight_zero_point = jax.random.uniform(k4, (512, 1), dtype=jnp.float32) * 63.0
        bias = jax.random.normal(k5, (512,), dtype=jnp.float32)
        return {'x': x, 'qweight': qweight, 'weight_scale': weight_scale, 'weight_zero_point': weight_zero_point, 'bias': bias}
    _L1_ffn_in = _L1_ffn_setup()
    _d = {'L0_attn_x': _L0_attn_in['x'], 'L0_attn_wq': _L0_attn_in['wq'], 'L0_attn_wk': _L0_attn_in['wk'], 'L0_attn_wv': _L0_attn_in['wv'], 'L0_attn_wo': _L0_attn_in['wo'], 'L0_ffn_w_gate': _L0_ffn_in['w_gate'], 'L0_ffn_b_gate': _L0_ffn_in['b_gate'], 'L0_ffn_w_up': _L0_ffn_in['w_up'], 'L0_ffn_b_up': _L0_ffn_in['b_up'], 'L0_ffn_w_down': _L0_ffn_in['w_down'], 'L0_ffn_b_down': _L0_ffn_in['b_down'], 'L1_attn_wq': _L1_attn_in['wq'], 'L1_attn_wk': _L1_attn_in['wk'], 'L1_attn_wv': _L1_attn_in['wv'], 'L1_attn_wo': _L1_attn_in['wo'], 'L1_ffn_qweight': _L1_ffn_in['qweight'], 'L1_ffn_weight_scale': _L1_ffn_in['weight_scale'], 'L1_ffn_weight_zero_point': _L1_ffn_in['weight_zero_point'], 'L1_ffn_bias': _L1_ffn_in['bias']}
    _x0 = _d['L0_attn_x']
    _d['L0_attn_x'] = jax.random.normal(jax.random.fold_in(jax.random.key(seed), 1), (4, 512, 512), dtype=_x0.dtype)
    del _x0
    return _d

def reference(L0_attn_x, L0_attn_wq, L0_attn_wk, L0_attn_wv, L0_attn_wo, L0_ffn_w_gate, L0_ffn_b_gate, L0_ffn_w_up, L0_ffn_b_up, L0_ffn_w_down, L0_ffn_b_down, L1_attn_wq, L1_attn_wk, L1_attn_wv, L1_attn_wo, L1_ffn_qweight, L1_ffn_weight_scale, L1_ffn_weight_zero_point, L1_ffn_bias):

    def _L0_attn_ref(x, wq, wk, wv, wo):
        import jax, jax.numpy as jnp
        import numpy as np
        B, S, D = (2, 256, 512)
        NH, NKV = (32, 8)
        HD = D // NH
        NREP = NH // NKV
        SCALE = HD ** (-0.5)
        b, s, _ = x.shape
        q = (x @ wq).reshape(b, s, NH, HD)
        k = (x @ wk).reshape(b, s, NKV, HD)
        v = (x @ wv).reshape(b, s, NKV, HD)
        k = jnp.repeat(k, NREP, axis=2)
        v = jnp.repeat(v, NREP, axis=2)
        scores = jnp.einsum('bihd,bjhd->bhij', q, k) * SCALE
        causal = jnp.tril(jnp.ones((s, s), dtype=bool))
        scores = jnp.where(causal, scores, jnp.finfo(scores.dtype).min)
        attn = jax.nn.softmax(scores, axis=-1)
        out = jnp.einsum('bhij,bjhd->bihd', attn, v)
        out = out.reshape(b, s, NH * HD)
        return out @ wo

    def _L0_ffn_ref(hidden_states, w_gate, b_gate, w_up, b_up, w_down, b_down):
        import jax, jax.numpy as jnp
        import numpy as np
        HIDDEN = 512
        INTER = 1376
        BATCH, SEQ = (2, 256)
        gate = jax.nn.silu(jnp.einsum('bsh,ih->bsi', hidden_states, w_gate) + b_gate)
        up = jnp.einsum('bsh,ih->bsi', hidden_states, w_up) + b_up
        return jnp.einsum('bsi,hi->bsh', gate * up, w_down) + b_down

    def _L1_attn_ref(x, wq, wk, wv, wo):
        import jax, jax.numpy as jnp
        import numpy as np
        H, KV, HD, HID = (32, 8, 128, 512)
        THETA, FACTOR, HI_FF, LO_FF, ORIG_MAX = (500000.0, 8.0, 4.0, 1.0, 1024)

        def _llama3_inv_freq():
            inv = 1.0 / THETA ** (np.arange(0, HD, 2, dtype=np.float64) / HD)
            wavelen = 2.0 * np.pi / inv
            low_wl = ORIG_MAX / LO_FF
            high_wl = ORIG_MAX / HI_FF
            smooth = (ORIG_MAX / wavelen - LO_FF) / (HI_FF - LO_FF)
            scaled = np.where(wavelen > low_wl, inv / FACTOR, inv)
            mid = (wavelen <= low_wl) & (wavelen >= high_wl)
            scaled = np.where(mid, (1 - smooth) * inv / FACTOR + smooth * inv, scaled)
            return scaled.astype(np.float32)

        def _rope_cos_sin(T):
            inv = _llama3_inv_freq()
            pos = np.arange(T, dtype=np.float32)
            freqs = pos[:, None] * inv[None, :]
            emb = np.concatenate([freqs, freqs], axis=-1)
            return (jnp.asarray(np.cos(emb)), jnp.asarray(np.sin(emb)))

        def _rotate_half(x):
            x1, x2 = jnp.split(x, 2, axis=-1)
            return jnp.concatenate([-x2, x1], axis=-1)
        B, T, _ = x.shape
        q = (x @ wq).reshape(B, T, H, HD).transpose(0, 2, 1, 3)
        k = (x @ wk).reshape(B, T, KV, HD).transpose(0, 2, 1, 3)
        v = (x @ wv).reshape(B, T, KV, HD).transpose(0, 2, 1, 3)
        cos, sin = _rope_cos_sin(T)
        q = q * cos + _rotate_half(q) * sin
        k = k * cos + _rotate_half(k) * sin
        rep = H // KV
        k = jnp.repeat(k, rep, axis=1)
        v = jnp.repeat(v, rep, axis=1)
        scores = jnp.einsum('bhtd,bhsd->bhts', q, k) * (1.0 / np.sqrt(HD))
        mask = jnp.tril(jnp.ones((T, T), dtype=bool))
        scores = jnp.where(mask, scores, -jnp.inf)
        att = jax.nn.softmax(scores, axis=-1)
        out = jnp.einsum('bhts,bhsd->bhtd', att, v)
        out = out.transpose(0, 2, 1, 3).reshape(B, T, H * HD)
        return out @ wo

    def _L1_ffn_ref(x, qweight, weight_scale, weight_zero_point, bias):
        import jax, jax.numpy as jnp
        import numpy as np
        IN_FEATURES = 512

        def _dequantize(qweight, scale, zero_point):
            N, K_packed = qweight.shape
            groups = K_packed // 3
            p = qweight.reshape(N, groups, 3)
            v0 = p[:, :, 0] & 63
            v1 = p[:, :, 0] >> 6 & 63
            v2 = p[:, :, 1] & 63
            v3 = p[:, :, 2] & 63
            unpacked = jnp.stack([v0, v1, v2, v3], axis=2).reshape(N, groups * 4)
            unpacked = unpacked[:, :IN_FEATURES]
            return (unpacked.astype(jnp.float32) - zero_point) * scale
        w = _dequantize(qweight, weight_scale, weight_zero_point)
        return jnp.einsum('bsk,nk->bsn', x, w) + bias
    x = L0_attn_x
    x = x + 0.5 * _L0_ffn_ref(_layernorm(x, axis=-1), L0_ffn_w_gate, L0_ffn_b_gate, L0_ffn_w_up, L0_ffn_b_up, L0_ffn_w_down, L0_ffn_b_down)
    x = x + _L0_attn_ref(_layernorm(x, axis=-1), L0_attn_wq, L0_attn_wk, L0_attn_wv, L0_attn_wo)
    x = x + 0.5 * _L0_ffn_ref(_layernorm(x, axis=-1), L0_ffn_w_gate, L0_ffn_b_gate, L0_ffn_w_up, L0_ffn_b_up, L0_ffn_w_down, L0_ffn_b_down)
    x = x + 0.5 * _L1_ffn_ref(_layernorm(x, axis=-1), L1_ffn_qweight, L1_ffn_weight_scale, L1_ffn_weight_zero_point, L1_ffn_bias)
    x = x + _L1_attn_ref(_layernorm(x, axis=-1), L1_attn_wq, L1_attn_wk, L1_attn_wv, L1_attn_wo)
    x = x + 0.5 * _L1_ffn_ref(_layernorm(x, axis=-1), L1_ffn_qweight, L1_ffn_weight_scale, L1_ffn_weight_zero_point, L1_ffn_bias)
    return x

_drawn_inputs = setup_inputs


def setup_inputs(seed=0):
    import zlib

    import numpy as np

    out = dict(_drawn_inputs(seed))
    spreads = {}
    factors = {'L0_attn_wq': 8.0,
     'L0_attn_wk': 8.0,
     'L0_ffn_b_gate': 8.0,
     'L0_ffn_b_up': 8.0,
     'L0_ffn_b_down': 2.761,
     'L1_ffn_weight_zero_point': 8.0}
    for name, (base, spread) in spreads.items():
        noise = np.random.default_rng([zlib.crc32(name.encode()), seed]).standard_normal(out[name].shape)
        drawn = base * np.exp(spread * noise) if base else spread * noise
        out[name] = jnp.asarray(drawn.astype(out[name].dtype))
    for name, factor in factors.items():
        out[name] = (out[name] * factor).astype(out[name].dtype)
    return out
```

```python
from contextlib import ExitStack

import numpy as np

import concourse.bass as bass
from concourse import mybir

F32 = mybir.dt.float32
F32R = mybir.dt.float32r
BF16 = mybir.dt.bfloat16
I32 = mybir.dt.int32
ALU = mybir.AluOpType
ACT = mybir.ActivationFunctionType
AX = mybir.AxisListType
ds = bass.ds

P = 128
BATCH, SEQ, D = 4, 512, 512
TOK = BATCH * SEQ
NT = TOK // P
TB = SEQ // P
C = D // P
EPS = 1e-5
RSQRT_MAGIC = float(0x5F3759DF)

INTER = 1376
IT = 11
I_LAST = INTER - (IT - 1) * P
FFN_M = 2 * C * P + D
FFN_W = FFN_M + 2

H0, HD0 = 32, 16
KV0 = 8
UH = P // HD0
UKV = UH * KV0 // H0
UNITS0 = H0 // UH * BATCH
QCOL = 2 * UKV * HD0
QKV0_W = C * (QCOL + P)
VWIN = 2 * P - HD0

HD1 = 128
G1, R1 = 8, 4
UNITS1 = G1 * BATCH
PIECES = 2 + 2 * R1

NEG = -1e30
QORDER = (3, 2, 0, 1)
SBANK = {3: (2, 0), 2: (1, 0), 0: (0, 0), 1: (0, 256)}
SWIDE = {0: 256, 1: 256, 2: 384, 3: 512}
POFF = {0: 0, 1: 256, 2: 512, 3: 896}
PWIDE = 1408
TBANK = {"A": 3, "B": 4, "C": 0}
OBANK = 6
WBANK = (5, 7)


def after(eng, sem, count):
    if not (isinstance(count, int) and count <= 0):
        eng.wait_ge(sem, count)


class Norm:

    def __init__(self, sem, tag):
        self.chain = sem(f"{tag}_stat")
        self.normed = sem(f"{tag}_normed")
        self.turned = sem(f"{tag}_turned")
        self.hi = sem(f"{tag}_hi")
        self.lo = sem(f"{tag}_lo")
        self.biased = sem(f"{tag}_biased")


class Program:
    def __init__(self, nc, io):
        self.nc, self.io = nc, io
        self.ctx = ExitStack()
        with self.ctx:
            self.place()
            self.run()

    def place(self):
        nc, keep = self.nc, self.ctx

        def sem(name):
            return keep.enter_context(nc.semaphore(name))

        def tensor(stack, name, shape, dt=F32):
            return stack.enter_context(nc.sbuf_tensor(name, shape, dt))

        self.sem = sem
        self.ps = keep.enter_context(nc.psum_tensor("ps", [P, 8, 512], F32))
        self.x = tensor(keep, "x", [P, NT, D])
        self.xh = tensor(keep, "xh", [P, C, TOK], F32R)
        self.xl = tensor(keep, "xl", [P, C, TOK], F32R)
        self.ident = tensor(keep, "ident", [P, P])
        self.identb = tensor(keep, "identb", [P, P], BF16)
        self.maskb = tensor(keep, "maskb", [P, P], BF16)

        with ExitStack() as s:
            self.n_xn = tensor(s, "n_xn", [P, TB, D])
            self.n_st = tensor(s, "n_st", [P, TB, 6])
            self.n_mv = tensor(s, "n_mv", [P, TB, 2])
            self.n_v = tensor(s, "n_v", [P, TB])
            self.n_y = tensor(s, "n_y", [P, TB])
            self.n_t = tensor(s, "n_t", [P, TB])
            self.hb = tensor(s, "hb", [P, D])
            self.hbraw = tensor(s, "hbraw", [P, D])
            with ExitStack() as f:
                self.f_raw = tensor(f, "f_raw", [P, 2, FFN_W])
                self.f_hi = tensor(f, "f_hi", [P, 2, FFN_M], F32R)
                self.f_lo = tensor(f, "f_lo", [P, 2, FFN_M], F32R)
                self.f_bias = tensor(f, "f_bias", [P, 2, 2])
                self.f_zero = tensor(f, "f_zero", [P, D + 2])
                self.f_silu = tensor(f, "f_silu", [P, 2, SEQ])
                self.f_h = tensor(f, "f_h", [P, 2, SEQ])
                self.f_hh = tensor(f, "f_hh", [P, 2, SEQ], F32R)
                self.f_hl = tensor(f, "f_hl", [P, 2, SEQ], F32R)
            with ExitStack() as f:
                self.d_q = tensor(f, "d_q", [P, 3, D], I32)
                self.d_u = tensor(f, "d_u", [P, C, D], I32)
                self.d_zp = tensor(f, "d_zp", [P, D])
                self.d_sc = tensor(f, "d_sc", [P, D])
                self.d_w = tensor(f, "d_w", [P, C, D])
                self.d_wh = tensor(f, "d_wh", [P, C, D], F32R)
                self.d_wl = tensor(f, "d_wl", [P, C, D], F32R)
        with ExitStack() as s:
            self.p = tensor(s, "p", [P, PWIDE])
            self.pth = tensor(s, "pth", [P, TB, SEQ], F32R)
            self.ptl = tensor(s, "ptl", [P, TB, SEQ], F32R)
            self.nmax = tensor(s, "nmax", [P, TB])
            self.psum_ = tensor(s, "psums", [P, TB])
            self.rsum = tensor(s, "rsum", [P, TB])
            with ExitStack() as f:
                self.a_rawqkv = tensor(f, "a_rawqkv", [P, QKV0_W])
                self.a_rawo = tensor(f, "a_rawo", [P, D])
                self.a_wh = tensor(f, "a_wh", [P, QKV0_W], F32R)
                self.a_wl = tensor(f, "a_wl", [P, QKV0_W], F32R)
                self.a_oh = tensor(f, "a_oh", [P, D], F32R)
                self.a_ol = tensor(f, "a_ol", [P, D], F32R)
                self.a_qh = tensor(f, "a_qh", [P, SEQ], F32R)
                self.a_ql = tensor(f, "a_ql", [P, SEQ], F32R)
                self.a_kh = tensor(f, "a_kh", [P, SEQ], F32R)
                self.a_kl = tensor(f, "a_kl", [P, SEQ], F32R)
                self.a_vt = tensor(f, "a_vt", [P, SEQ])
                self.a_q2 = tensor(f, "a_q2", [P, 2, UH // 2, SEQ], F32R)
                self.a_k2 = tensor(f, "a_k2", [P, 2, 2, UKV, SEQ], F32R)
                self.a_vh = tensor(f, "a_vh", [P, UKV, TB, VWIN], F32R)
                self.a_vl = tensor(f, "a_vl", [P, UKV, TB, VWIN], F32R)
                self.a_oth = tensor(f, "a_oth", [P, SEQ], F32R)
                self.a_otl = tensor(f, "a_otl", [P, SEQ], F32R)
            with ExitStack() as f:
                self.r_raw = tensor(f, "r_raw", [P, 512])
                self.r_wh = tensor(f, "r_wh", [P, PIECES, 512], F32R)
                self.r_wl = tensor(f, "r_wl", [P, PIECES, 512], F32R)
                self.r_cos = tensor(f, "r_cos", [P, SEQ])
                self.r_sin = tensor(f, "r_sin", [P, SEQ])
                self.r_t = tensor(f, "r_t", [P, SEQ])
                self.r_sw = tensor(f, "r_sw", [P, SEQ])
                self.r_qh = tensor(f, "r_qh", [P, 2, SEQ], F32R)
                self.r_ql = tensor(f, "r_ql", [P, 2, SEQ], F32R)
                self.r_kh = tensor(f, "r_kh", [P, 2, SEQ], F32R)
                self.r_kl = tensor(f, "r_kl", [P, 2, SEQ], F32R)
                self.r_vt = tensor(f, "r_vt", [P, SEQ])
                self.r_vh = tensor(f, "r_vh", [P, TB, HD1], F32R)
                self.r_vl = tensor(f, "r_vl", [P, TB, HD1], F32R)
                self.r_oth = tensor(f, "r_oth", [P, R1, SEQ], F32R)
                self.r_otl = tensor(f, "r_otl", [P, R1, SEQ], F32R)

        self.x_in = sem("x_in")
        self.consts = sem("consts")
        self.x_out = sem("x_out")

    def run(self):
        io = self.io
        gated = dict(w=io["ffn_w"], w_gu_last=io["ffn_gu_last"], w_d_last=io["ffn_d_last"],
                     out_bias=io["ffn_bd"])
        deq = dict(q=io["deq_q"], zp=io["deq_zp"], sc=io["deq_sc"], out_bias=io["deq_b"])
        stages = [
            GatedFfn(self, "fa", **gated), SmallHeads(self, "at"), GatedFfn(self, "fb", **gated),
            DequantFfn(self, "da", **deq), RopeHeads(self, "ro"), DequantFfn(self, "db", **deq),
        ]
        for prev, s in zip([None] + stages, stages):
            s.prev = prev
        last = stages[-1]
        nc = self.nc
        block = self.ctx.enter_context(nc.Block())

        @block.sync
        def _(sp):
            for b in range(BATCH):
                sp.dma_start(self.x[:, TB * b:TB * b + TB, :],
                             io["x"][SEQ * b:SEQ * b + SEQ, :].rearrange("(t p) d -> p t d", p=P)
                             ).then_inc(self.x_in, 16)
            for s in stages:
                s.sync(sp)
            for m in range(NT):
                sp.wait_ge(last.x_new, last.tile_ready(m))
                sp.dma_start(io["out"][P * m:P * m + P, :], self.x[:, m, :]).then_inc(self.x_out, 16)
            sp.wait_ge(self.x_out, 16 * NT)

        @block.gpsimd
        def _(pool):
            nc.gpsimd.memset(self.ident[:], 0.0).then_inc(self.consts, 1)
            nc.gpsimd.memset(self.maskb[:], 0.0).then_inc(self.consts, 1)
            pool.wait_ge(self.consts, 2)
            nc.gpsimd.affine_select(out=self.ident[:], in_=self.ident[:], compare_op=ALU.not_equal,
                                    fill=1.0, base=0, pattern=[[-1, P]],
                                    channel_multiplier=1).then_inc(self.consts, 1)
            nc.gpsimd.affine_select(out=self.maskb[:], in_=self.maskb[:], compare_op=ALU.is_ge,
                                    fill=NEG, base=0, pattern=[[-1, P]],
                                    channel_multiplier=1).then_inc(self.consts, 1)
            pool.wait_ge(self.consts, 4)
            nc.gpsimd.tensor_copy(self.identb[:], self.ident[:]).then_inc(self.consts, 1)
            for s in stages:
                s.gpsimd(pool)

        @block.scalar
        def _(act):
            for s in stages:
                s.scalar(act)

        @block.vector
        def _(dve):
            for s in stages:
                s.vector(dve)

        @block.tensor
        def _(pe):
            pe.wait_ge(self.consts, 5)
            for s in stages:
                s.tensor(pe)

    def norm_vector(self, dve, s):
        nc, nm = self.nc, s.norm
        n = 0

        def step(ins):
            nonlocal n
            n += 1
            ins.then_inc(nm.chain, 1)

        if s.prev is None:
            dve.wait_ge(self.x_in, 16 * BATCH)
        else:
            dve.wait_ge(s.prev.x_new, s.prev.x_new_total)
        for b in range(BATCH):
            for j in range(TB):
                step(nc.vector.bn_stats(self.n_st[:, j, :], self.x[:, TB * b + j, :]))
            for j in range(TB):
                dve.wait_ge(nm.chain, n - TB + 1)
                step(nc.vector.bn_aggr(self.n_mv[:, j, :], self.n_st[:, j, :]))
            dve.wait_ge(nm.chain, n)
            step(nc.vector.tensor_scalar(self.n_v[:], self.n_mv[:, :, 1], EPS, None, ALU.add))
            dve.wait_ge(nm.chain, n)
            step(nc.vector.tensor_scalar(self.n_y[:].bitcast(I32), self.n_v[:].bitcast(I32), -0.5,
                                         RSQRT_MAGIC, ALU.mult, ALU.add))
            for _ in range(4):
                dve.wait_ge(nm.chain, n)
                step(nc.vector.scalar_tensor_tensor(out=self.n_t[:], in0=self.n_y[:], scalar=-0.5,
                                                    in1=self.n_y[:], op0=ALU.mult, op1=ALU.mult))
                dve.wait_ge(nm.chain, n)
                step(nc.vector.tensor_tensor(self.n_t[:], self.n_t[:], self.n_v[:], ALU.mult))
                dve.wait_ge(nm.chain, n)
                step(nc.vector.scalar_tensor_tensor(out=self.n_y[:], in0=self.n_t[:], scalar=1.5,
                                                    in1=self.n_y[:], op0=ALU.add, op1=ALU.mult))
            dve.wait_ge(nm.chain, n)
            for j in range(TB):
                m = TB * b + j
                after(dve, nm.turned, m - TB + 1)
                nc.vector.tensor_scalar(self.n_xn[:, j, :], self.x[:, m, :], self.n_mv[:, j, 0:1],
                                        self.n_y[:, j:j + 1], ALU.subtract,
                                        ALU.mult).then_inc(nm.normed, 1)
            for j in range(TB):
                m = TB * b + j
                dve.wait_ge(nm.hi, m + 1)
                nc.vector.tensor_tensor(
                    self.xl[:, :, P * m:P * m + P], self.ps[:, s.NORM_BANK + m % 4, :].rearrange("p (c t) -> p c t", c=C),
                    self.xh[:, :, P * m:P * m + P].bitcast(F32), ALU.subtract).then_inc(nm.lo, 1)

    def norm_tensor(self, pe, s):
        nc, nm = self.nc, s.norm
        for m in range(NT):
            pe.wait_ge(nm.normed, m + 1)
            after(pe, nm.lo, m - 3)
            for c in range(C):
                last = nc.tensor.transpose(self.ps[:, s.NORM_BANK + m % 4, P * c:P * c + P],
                                           self.n_xn[:, m % TB, c::C], self.ident[:])
            last.then_inc(nm.turned, 1)

    def norm_scalar(self, act, s):
        nc, nm = self.nc, s.norm
        for m in range(NT):
            act.wait_ge(nm.turned, m + 1)
            nc.scalar.copy(self.xh[:, :, P * m:P * m + P],
                           self.ps[:, s.NORM_BANK + m % 4, :].rearrange("p (c t) -> p c t", c=C)).then_inc(nm.hi, 1)

    def norm_gpsimd(self, pool, s):
        nc, nm = self.nc, s.norm
        pool.wait_ge(s.bias_in, 16)
        nc.gpsimd.tensor_scalar(self.hb[:], self.hbraw[:], 0.5, None, ALU.mult).then_inc(s.halved, 1)
        pool.wait_ge(s.halved, 1)
        for m in range(NT):
            pool.wait_ge(nm.normed, m + 1)
            nc.gpsimd.tensor_tensor(self.x[:, m, :], self.x[:, m, :], self.hb[:],
                                    ALU.add).then_inc(nm.biased, 1)


class GatedFfn:

    STEPS = IT * BATCH
    x_new_total = STEPS * TB
    NORM_BANK = 4

    def __init__(self, pr, tag, w, w_gu_last, w_d_last, out_bias):
        self.pr, self.nc = pr, pr.nc
        self.w, self.w_gu_last, self.w_d_last = w, w_gu_last, w_d_last
        self.out_bias = out_bias
        sem = pr.sem
        self.norm = Norm(sem, f"{tag}_norm")
        self.bias_in = sem(f"{tag}_bias_in")
        self.halved = sem(f"{tag}_halved")
        self.small = sem(f"{tag}_small")
        self.zeroed = sem(f"{tag}_zeroed")
        self.tail = sem(f"{tag}_tail")
        self.raw = [sem(f"{tag}_raw{i}") for i in range(2)]
        self.w_hi = sem(f"{tag}_w_hi")
        self.w_lo = sem(f"{tag}_w_lo")
        self.gu = sem(f"{tag}_gu")
        self.silu = sem(f"{tag}_silu")
        self.h = sem(f"{tag}_h")
        self.h_hi = sem(f"{tag}_h_hi")
        self.h_lo = sem(f"{tag}_h_lo")
        self.down = sem(f"{tag}_down")
        self.x_new = sem(f"{tag}_x_new")

    def tile_ready(self, m):
        return self.x_new_total - NT + m + 1

    def gate_cols(self, c):
        return slice(P * c, P * c + P)

    def up_cols(self, c):
        return slice(P * (C + c), P * (C + c) + P)

    def sync(self, sp):
        pr = self.pr
        if self.prev is not None:
            sp.wait_ge(self.prev.x_new, self.prev.x_new_total)
        sp.dma_start(pr.hbraw[:], self.out_bias.partition_broadcast(P)).then_inc(self.bias_in, 16)
        for i in range(2):
            sp.dma_start(pr.f_raw[:, i, :], self.w[i]).then_inc(self.raw[i], 16)
        with sp.Fori(0, 4) as k:
            for par in range(2):
                sp.wait_ge(self.w_lo, k * 2 + (par + 1))
                sp.dma_start(pr.f_raw[:, par, :],
                             self.w[ds(k * 2 + (par + 2), 1)].rearrange("o p n -> p (o n)")
                             ).then_inc(self.raw[par], 16)
        gu = pr.f_raw[:, 0, 0:2 * C * P].rearrange("p (c n) -> p c n", n=P)
        down = slice(2 * C * P, FFN_W)
        sp.wait_ge(self.w_lo, IT - 2)
        sp.wait_ge(self.zeroed, 1)
        sp.dma_start(gu[:, :, I_LAST:P], pr.f_zero[:, 0:2 * C * (P - I_LAST)].rearrange(
            "p (c n) -> p c n", c=2 * C)).then_inc(self.tail, 16)
        sp.dma_start(pr.f_raw[I_LAST:P, 0, down], pr.f_zero[I_LAST:P, :]).then_inc(self.tail, 16)
        sp.dma_start(pr.f_raw[0:I_LAST, 0, down], self.w_d_last).then_inc(self.tail, 16)
        sp.wait_ge(self.tail, 48)
        sp.dma_start(gu[:, :, 0:I_LAST], self.w_gu_last).then_inc(self.raw[0], 16)

    def weights_hi(self, act, i, par, loads):
        act.wait_ge(self.raw[par], loads)
        after(act, self.down, i * 16 - 16)
        self.nc.scalar.copy(self.pr.f_bias[:, par, :], self.pr.f_raw[:, par, FFN_M:]).then_inc(self.small, 1)
        self.nc.scalar.copy(self.pr.f_hi[:, par, :], self.pr.f_raw[:, par, 0:FFN_M]).then_inc(self.w_hi, 1)

    def weights_lo(self, pool, i, par):
        pr = self.pr
        pool.wait_ge(self.w_hi, i + 1)
        self.nc.gpsimd.tensor_tensor(pr.f_lo[:, par, :], pr.f_raw[:, par, 0:FFN_M],
                                     pr.f_hi[:, par, :].bitcast(F32), ALU.subtract).then_inc(self.w_lo, 1)

    def gate_up(self, pe, t, i, s):
        pr, par, b, hp = self.pr, s // 4 % 2, s % 4, s % 2
        if b == 0:
            pe.wait_ge(self.w_lo, i + 1)
        if isinstance(t, int) and t < 4:
            pe.wait_ge(self.norm.lo, TB * (b + 1))
        after(pe, self.h, t - 1)
        tok = slice(SEQ * b, SEQ * b + SEQ)
        for bank, cols in ((2 * hp, self.gate_cols), (2 * hp + 1, self.up_cols)):
            for c in range(C):
                for a, w, x in ((0, pr.f_hi, pr.xh), (1, pr.f_hi, pr.xl), (2, pr.f_lo, pr.xh)):
                    last = self.nc.tensor.matmul(pr.ps[:, bank, :], w[:, par, cols(c)], x[:, c, tok],
                                                 start=(c == 0 and a == 0), stop=(c == C - 1 and a == 2))
        last.then_inc(self.gu, 1)

    def down_rows(self, pe, t, s):
        pr, par, hp = self.pr, s // 4 % 2, s % 2
        pe.wait_ge(self.h_lo, t + 1)
        if isinstance(t, int) and t == 0:
            pe.wait_ge(self.norm.lo, NT)
        for j in range(TB):
            after(pe, self.x_new, t * 4 + (j - 3))
            tok = slice(P * j, P * j + P)
            down = slice(2 * C * P, FFN_M)
            for a, h, w in ((0, pr.f_hh, pr.f_hi), (1, pr.f_hh, pr.f_lo), (2, pr.f_hl, pr.f_hi)):
                last = self.nc.tensor.matmul(pr.ps[:, 4 + j, :], h[:, hp, tok], w[:, par, down],
                                             start=(a == 0), stop=(a == 2))
            last.then_inc(self.down, 1)

    def tensor(self, pe):
        self.pr.norm_tensor(pe, self)
        self.gate_up(pe, 0, 0, 0)
        for s in range(8):
            self.gate_up(pe, s + 1, (s + 1) // 4, (s + 1) % 8)
            self.down_rows(pe, s, s)
        with pe.Fori(1, IT // 2) as k:
            for s in range(8):
                self.gate_up(pe, k * 8 + (s + 1), k * 2 + (s + 1) // 4, (s + 1) % 8)
                self.down_rows(pe, k * 8 + s, s)
        for s in range(4):
            t = self.STEPS - 4 + s
            if s < 3:
                self.gate_up(pe, t + 1, IT - 1, s + 1)
            self.down_rows(pe, t, s)

    def act_step(self, act, t, i, s):
        pr, b, hp = self.pr, s % 4, s % 2
        if b == 0:
            act.wait_ge(self.small, i + 1)
        act.wait_ge(self.gu, t + 1)
        after(act, self.h, t - 1)
        self.nc.scalar.activation(pr.f_silu[:, hp, :], pr.ps[:, 2 * hp, :], ACT.Silu,
                                  bias=pr.f_bias[:, s // 4 % 2, 0:1]).then_inc(self.silu, 1)
        act.wait_ge(self.h, t + 1)
        after(act, self.down, t * 4 - 4)
        self.nc.scalar.copy(pr.f_hh[:, hp, :], pr.f_h[:, hp, :]).then_inc(self.h_hi, 1)

    def scalar(self, act):
        self.pr.norm_scalar(act, self)
        self.weights_hi(act, 0, 0, 16)
        self.weights_hi(act, 1, 1, 16)
        for s in range(8):
            self.act_step(act, s, s // 4, s)
            if s == 5:
                self.weights_hi(act, 2, 0, 32)
        with act.Fori(1, IT // 2) as k:
            for s in range(8):
                self.act_step(act, k * 8 + s, k * 2 + s // 4, s)
                if s == 1:
                    self.weights_hi(act, k * 2 + 1, 1, k * 16 + 16)
                if s == 5:
                    self.weights_hi(act, k * 2 + 2, 0, k * 16 + 32)
        for s in range(4):
            self.act_step(act, self.STEPS - 4 + s, IT - 1, s)

    def vec_h(self, dve, t, i, s):
        pr, hp = self.pr, s % 2
        dve.wait_ge(self.silu, t + 1)
        after(dve, self.h_lo, t - 1)
        self.nc.vector.scalar_tensor_tensor(out=pr.f_h[:, hp, :], in0=pr.ps[:, 2 * hp + 1, :],
                                            scalar=pr.f_bias[:, s // 4 % 2, 1:2], in1=pr.f_silu[:, hp, :],
                                            op0=ALU.add, op1=ALU.mult).then_inc(self.h, 1)

    def vec_x(self, dve, t, s):
        pr, b = self.pr, s % 4
        for j in range(TB):
            dve.wait_ge(self.down, t * 4 + (j + 1))
            xm = pr.x[:, TB * b + j, :]
            self.nc.vector.scalar_tensor_tensor(out=xm, in0=pr.ps[:, 4 + j, :], scalar=0.5, in1=xm,
                                                op0=ALU.mult, op1=ALU.add).then_inc(self.x_new, 1)

    def vector(self, dve):
        self.pr.norm_vector(dve, self)
        dve.wait_ge(self.norm.biased, NT)
        self.vec_h(dve, 0, 0, 0)
        for s in range(8):
            self.vec_h(dve, s + 1, (s + 1) // 4, (s + 1) % 8)
            self.vec_x(dve, s, s)
        with dve.Fori(1, IT // 2) as k:
            for s in range(8):
                self.vec_h(dve, k * 8 + (s + 1), k * 2 + (s + 1) // 4, (s + 1) % 8)
                self.vec_x(dve, k * 8 + s, s)
        for s in range(4):
            t = self.STEPS - 4 + s
            if s < 3:
                self.vec_h(dve, t + 1, IT - 1, s + 1)
            self.vec_x(dve, t, s)

    def pool_step(self, pool, t, s):
        pr, hp = self.pr, s % 2
        pool.wait_ge(self.h_hi, t + 1)
        self.nc.gpsimd.tensor_tensor(pr.f_hl[:, hp, :], pr.f_h[:, hp, :], pr.f_hh[:, hp, :].bitcast(F32),
                                     ALU.subtract).then_inc(self.h_lo, 1)

    def gpsimd(self, pool):
        nc, pr = self.nc, self.pr
        if self.prev is not None:
            pool.wait_ge(self.prev.x_new, self.prev.x_new_total)
        nc.gpsimd.memset(pr.f_zero[:], 0.0).then_inc(self.zeroed, 1)
        self.weights_lo(pool, 0, 0)
        self.weights_lo(pool, 1, 1)
        pr.norm_gpsimd(pool, self)
        for s in range(8):
            self.pool_step(pool, s, s)
            if s == 5:
                self.weights_lo(pool, 2, 0)
        with pool.Fori(1, IT // 2) as k:
            for s in range(8):
                self.pool_step(pool, k * 8 + s, s)
                if s == 1:
                    self.weights_lo(pool, k * 2 + 1, 1)
                if s == 5:
                    self.weights_lo(pool, k * 2 + 2, 0)
        for s in range(4):
            self.pool_step(pool, self.STEPS - 4 + s, s)


class DequantFfn:

    x_new_total = NT
    NORM_BANK = 0
    BANKS = (4, 5, 6, 7)

    def __init__(self, pr, tag, q, zp, sc, out_bias):
        self.pr, self.nc = pr, pr.nc
        self.q, self.zp, self.sc, self.out_bias = q, zp, sc, out_bias
        sem = pr.sem
        self.norm = Norm(sem, f"{tag}_norm")
        self.bias_in = sem(f"{tag}_bias_in")
        self.halved = sem(f"{tag}_halved")
        self.coded = sem(f"{tag}_coded")
        self.codes = sem(f"{tag}_codes")
        self.wsub = sem(f"{tag}_wsub")
        self.wmul = sem(f"{tag}_wmul")
        self.w_hi = sem(f"{tag}_w_hi")
        self.w_lo = sem(f"{tag}_w_lo")
        self.y = sem(f"{tag}_y")
        self.x_new = sem(f"{tag}_x_new")

    def tile_ready(self, m):
        return m + 1

    def sync(self, sp):
        pr = self.pr
        if self.prev is not None:
            sp.wait_ge(self.prev.x_new, self.prev.x_new_total)
        sp.dma_start(pr.hbraw[:], self.out_bias.partition_broadcast(P)).then_inc(self.bias_in, 16)
        sp.dma_start(pr.d_q[:], self.q).then_inc(self.coded, 16)
        sp.dma_start(pr.d_zp[:], self.zp.partition_broadcast(P)).then_inc(self.coded, 16)
        sp.dma_start(pr.d_sc[:], self.sc.partition_broadcast(P)).then_inc(self.coded, 16)

    def vector(self, dve):
        nc, pr = self.nc, self.pr
        dve.wait_ge(self.coded, 48)
        if self.prev is not None:
            dve.wait_ge(self.prev.x_new, self.prev.x_new_total)
        for c, (word, shift) in enumerate(((0, 0), (0, 6), (1, 0), (2, 0))):
            nc.vector.tensor_scalar(pr.d_u[:, c, :], pr.d_q[:, word, :], shift, 63,
                                    ALU.arith_shift_right, ALU.bitwise_and).then_inc(self.codes, 1)
        for c in range(C):
            dve.wait_ge(self.codes, c + 1)
            nc.vector.tensor_tensor(pr.d_w[:, c, :], pr.d_u[:, c, :], pr.d_zp[:],
                                    ALU.subtract).then_inc(self.wsub, 1)
        for c in range(C):
            dve.wait_ge(self.wsub, c + 1)
            nc.vector.tensor_tensor(pr.d_w[:, c, :], pr.d_w[:, c, :], pr.d_sc[:],
                                    ALU.mult).then_inc(self.wmul, 1)
        for c in range(C):
            dve.wait_ge(self.w_hi, c + 1)
            nc.vector.tensor_tensor(pr.d_wl[:, c, :], pr.d_w[:, c, :], pr.d_wh[:, c, :].bitcast(F32),
                                    ALU.subtract).then_inc(self.w_lo, 1)
        pr.norm_vector(dve, self)
        dve.wait_ge(self.norm.biased, NT)
        for m in range(NT):
            dve.wait_ge(self.y, m + 1)
            xm = pr.x[:, m, :]
            nc.vector.scalar_tensor_tensor(out=xm, in0=pr.ps[:, self.BANKS[m % 4], :], scalar=0.5,
                                           in1=xm, op0=ALU.mult, op1=ALU.add).then_inc(self.x_new, 1)

    def scalar(self, act):
        nc, pr = self.nc, self.pr
        for c in range(C):
            act.wait_ge(self.wmul, c + 1)
            nc.scalar.copy(pr.d_wh[:, c, :], pr.d_w[:, c, :]).then_inc(self.w_hi, 1)
        pr.norm_scalar(act, self)

    def gpsimd(self, pool):
        self.pr.norm_gpsimd(pool, self)

    def tensor(self, pe):
        nc, pr = self.nc, self.pr
        pr.norm_tensor(pe, self)
        pe.wait_ge(self.w_lo, C)
        for m in range(NT):
            pe.wait_ge(self.norm.lo, m + 1)
            after(pe, self.x_new, m - 3)
            tok = slice(P * m, P * m + P)
            for c in range(C):
                for a, x, w in ((0, pr.xh, pr.d_wh), (1, pr.xh, pr.d_wl), (2, pr.xl, pr.d_wh)):
                    last = nc.tensor.matmul(pr.ps[:, self.BANKS[m % 4], :], x[:, c, tok], w[:, c, :],
                                            start=(c == 0 and a == 0), stop=(c == C - 1 and a == 2))
            last.then_inc(self.y, 1)


class Heads:

    NORM_BANK = 3

    def __init__(self, pr, tag):
        self.pr, self.nc = pr, pr.nc
        sem = pr.sem
        self.norm = Norm(sem, f"{tag}_norm")
        self.zeroed = sem(f"{tag}_zeroed")
        self.score = sem(f"{tag}_score")
        self.max = sem(f"{tag}_max")
        self.exp = sem(f"{tag}_exp")
        self.inv = sem(f"{tag}_inv")
        self.prob = sem(f"{tag}_prob")
        self.turn = sem(f"{tag}_turn")
        self.p_hi = sem(f"{tag}_p_hi")
        self.p_lo = sem(f"{tag}_p_lo")
        self.out = sem(f"{tag}_out")
        self.o_hi = sem(f"{tag}_o_hi")
        self.o_lo = sem(f"{tag}_o_lo")
        self.work = sem(f"{tag}_work")
        self.taken = sem(f"{tag}_taken")
        self.x_new = self.taken

    def tile_ready(self, m):
        return self.x_new_total

    def scores(self, pe, n, products):
        pr, nc = self.pr, self.nc
        for i, q in enumerate(QORDER):
            bank, col = SBANK[q]
            if q == 0:
                after(pe, self.p_lo, n * 3)
            for a, (qt, kt) in enumerate(products):
                nc.tensor.matmul(pr.ps[:, bank, col:col + SWIDE[q]], qt[:, P * q:P * q + P],
                                 kt[:, 0:SWIDE[q]], start=(a == 0), stop=False)
            own = col + P * q
            nc.tensor.matmul(pr.ps[:, bank, own:own + P], pr.identb[:], pr.maskb[:], start=False,
                             stop=True).then_inc(self.score, 1)

    def turn_probs(self, pe, n):
        pr, nc = self.pr, self.nc

        def turn(bank, blocks):
            for at, q, k in blocks:
                src = POFF[q] + P * k
                last = nc.tensor.transpose(pr.ps[:, TBANK[bank], P * at:P * at + P],
                                           pr.p[:, src:src + P], pr.ident[:])
            last.then_inc(self.turn, 1)

        pe.wait_ge(self.prob, n * 4 + 1)
        turn("A", [(k, 3, k) for k in range(4)])
        pe.wait_ge(self.prob, n * 4 + 2)
        turn("B", [(k, 2, k) for k in range(3)])
        pe.wait_ge(self.prob, n * 4 + 4)
        turn("C", [(2 * k + q, q, k) for k in range(2) for q in range(2)])

    def attend(self, pe, n, v_hi, v_lo, first, end):
        pr, nc = self.pr, self.nc
        pe.wait_ge(self.p_lo, n * 3 + 3)
        for k in range(TB):
            lo = min(k, TB - 2) * P
            for a, v, p in ((0, v_hi, pr.pth), (1, v_lo, pr.pth), (2, v_hi, pr.ptl)):
                last = nc.tensor.matmul(pr.ps[:, OBANK, lo:SEQ], v(k), p[:, k, lo:SEQ],
                                        start=(first and k == 0 and a == 0),
                                        stop=(end and k == TB - 1 and a == 2))
        return last

    def maxima(self, dve, n):
        pr, nc = self.pr, self.nc
        for i, q in enumerate(QORDER):
            if i < 3:
                dve.wait_ge(self.score, n * 4 + (i + 1 if i < 2 else 4))
            bank, col = SBANK[q]
            nc.vector.tensor_reduce(pr.nmax[:, q:q + 1], pr.ps[:, bank, col:col + P * (q + 1)], AX.X,
                                    ALU.max, negate=True).then_inc(self.max, 1)

    def normalise(self, dve, n):
        pr, nc = self.pr, self.nc
        for i, tiles in enumerate(((3,), (2,), (0, 1))):
            dve.wait_ge(self.exp, n * 4 + (1, 2, 4)[i])
            a, b = tiles[0], tiles[-1] + 1
            nc.vector.reciprocal(pr.rsum[:, a:b], pr.psum_[:, a:b]).then_inc(self.inv, 1)
            dve.wait_ge(self.inv, n * 3 + (i + 1))
            for q in tiles:
                p = pr.p[:, POFF[q]:POFF[q] + P * (q + 1)]
                nc.vector.tensor_scalar(p, p, pr.rsum[:, q:q + 1], None, ALU.mult).then_inc(self.prob, 1)

    def turned_views(self, i, dst):
        ps = self.pr.ps
        if i == 0:
            return ps[:, TBANK["A"], :].rearrange("p (k t) -> p k t", k=4), dst[:, :, 3 * P:4 * P]
        if i == 1:
            return (ps[:, TBANK["B"], 0:3 * P].rearrange("p (k t) -> p k t", k=3), dst[:, 0:3, 2 * P:3 * P])
        return ps[:, TBANK["C"], :].rearrange("p (k t) -> p k t", k=2), dst[:, 0:2, 0:2 * P]

    def probs_lo(self, dve, n):
        pr = self.pr
        for i in range(3):
            dve.wait_ge(self.p_hi, n * 3 + (i + 1))
            src, lo = self.turned_views(i, pr.ptl)
            _, hi = self.turned_views(i, pr.pth)
            self.nc.vector.tensor_tensor(lo, src, hi.bitcast(F32), ALU.subtract).then_inc(self.p_lo, 1)

    def exponentials(self, act, n):
        pr, nc = self.pr, self.nc
        for i, q in enumerate(QORDER):
            if i < 3:
                act.wait_ge(self.max, n * 4 + (i + 1 if i < 2 else 4))
            bank, col = SBANK[q]
            w = P * (q + 1)
            nc.scalar.activation(pr.p[:, POFF[q]:POFF[q] + w], pr.ps[:, bank, col:col + w], ACT.Exp,
                                 bias=pr.nmax[:, q:q + 1],
                                 accum_out=pr.psum_[:, q:q + 1]).then_inc(self.exp, 1)

    def probs_hi(self, act, n):
        for i in range(3):
            act.wait_ge(self.turn, n * 3 + (i + 1))
            src, hi = self.turned_views(i, self.pr.pth)
            self.nc.scalar.copy(hi, src).then_inc(self.p_hi, 1)

    def clear(self, pool, more):
        pr, nc = self.pr, self.nc
        pool.wait_ge(self.norm.lo, NT)
        regions = [pr.p[:, P:2 * P], pr.pth[:, 3, 2 * P:3 * P].bitcast(F32),
                   pr.ptl[:, 3, 2 * P:3 * P].bitcast(F32)] + more
        for i, r in enumerate(regions):
            after(pool, self.zeroed, i)
            nc.gpsimd.memset(r, 0.0).then_inc(self.zeroed, 1)
        self.cleared = len(regions)

    def x_tile(self, m):
        return self.pr.x[:].rearrange("p t d -> p (t d)")[:, ds(m * D, D)]


class SmallHeads(Heads):

    x_new_total = UNITS0 * 7
    Q_SCALE = HD0 ** -0.5
    COPIES = UH * 4 + UKV * 8

    def __init__(self, pr, tag):
        super().__init__(pr, tag)
        sem = pr.sem
        self.qkv_in = sem(f"{tag}_qkv_in")
        self.qkv_hi = sem(f"{tag}_qkv_hi")
        self.qkv_lo = sem(f"{tag}_qkv_lo")
        self.wo_in = sem(f"{tag}_wo_in")
        self.wo_hi = sem(f"{tag}_wo_hi")
        self.wo_lo = sem(f"{tag}_wo_lo")
        self.q_hi = sem(f"{tag}_q_hi")
        self.k_hi = sem(f"{tag}_k_hi")
        self.v_hi = sem(f"{tag}_v_hi")
        self.spread = sem(f"{tag}_spread")

    @staticmethod
    def item(u, kind, j=0):
        if isinstance(u, int) and u == 0:
            return 2 + {"vt": 0, "q": 1, "kv": 2}[kind]
        return u * 7 + (-2 + {"vt": 0, "y": 1 + j, "q": 5, "kv": 6}[kind])

    def bank(self, ps_, kind, j=0):
        if kind == "first":
            return WBANK[j]
        return WBANK[(ps_ * 7 + {"vt": 0, "y": 1 + j, "q": 5, "kv": 6}[kind]) % 2]

    def x_of(self, u, part, c):
        col = (u & 3) * SEQ
        return part[:, c, ds(col, SEQ)]

    def project(self, pe, u, w, bank, cols):
        pr = self.pr
        pe.wait_ge(self.norm.lo, NT)
        after(pe, self.taken, w - 1)
        pe.wait_ge(self.qkv_lo, u + 1)
        step = QCOL + P
        for c in range(C):
            at = slice(step * c + cols, step * c + cols + P)
            for a, wt, x in ((0, pr.a_wh, pr.xh), (1, pr.a_wh, pr.xl), (2, pr.a_wl, pr.xh)):
                last = self.nc.tensor.matmul(pr.ps[:, bank, :], wt[:, at], self.x_of(u, x, c),
                                             start=(c == 0 and a == 0), stop=(c == C - 1 and a == 2))
        last.then_inc(self.work, 1)

    def turn_values(self, pe, u, w, bank, w_kv):
        pr = self.pr
        pe.wait_ge(pr.consts, 5)
        pe.wait_ge(self.taken, w_kv + 1)
        after(pe, self.taken, w - 1)
        for k in range(TB):
            last = self.nc.tensor.transpose(pr.ps[:, bank, P * k:P * k + P], pr.a_vt[:, P * k:P * k + P],
                                            pr.ident[:])
        last.then_inc(self.work, 1)

    def result(self, pe, u, w, bank, j):
        pr = self.pr
        if j == 0:
            pe.wait_ge(self.o_lo, u + 1)
            pe.wait_ge(self.wo_lo, u + 1)
        after(pe, self.taken, w - 1)
        tok = slice(P * j, P * j + P)
        for a, o, wt in ((0, pr.a_oth, pr.a_oh), (1, pr.a_oth, pr.a_ol), (2, pr.a_otl, pr.a_oh)):
            last = self.nc.tensor.matmul(pr.ps[:, bank, :], o[:, tok], wt[:], start=(a == 0), stop=(a == 2))
        last.then_inc(self.work, 1)

    def values(self, pe, n, u, j, vt_item):
        pr = self.pr
        if j == 0:
            pe.wait_ge(self.taken, vt_item + 1)
            after(pe, self.o_lo, u)
        at = VWIN - P - HD0 * j
        kv = j // (UH // UKV)
        last = self.attend(pe, n, lambda k: pr.a_vh[:, kv, k, at:at + P], lambda k: pr.a_vl[:, kv, k, at:at + P],
                           first=(j == 0), end=(j == UH - 1))
        if j == UH - 1:
            last.then_inc(self.out, 1)

    def unit_tensor(self, pe, u, par, first=False, last=False):
        pr = self.pr
        for j in range(UH):
            n = u * UH + j
            if j == 0:
                pe.wait_ge(self.spread, u * (16 * self.COPIES) + 16 * self.COPIES)
            self.scores(pe, n, [(pr.a_q2[:, par, j // 2, :], pr.a_k2[:, par, j % 2, j // (UH // UKV), :])])
            if j == 1 and not first:
                for t in range(TB):
                    self.result(pe, u - 1, self.item(u, "y", t), self.bank(par, "y", t), t)
            if j == 2 and not last:
                self.project(pe, u + 1, self.item(u, "q"), self.bank(par, "q"), QCOL)
            if j == 3 and not last:
                self.project(pe, u + 1, self.item(u, "kv"), self.bank(par, "kv"), 0)
            if j > 0:
                self.values(pe, n - 1, u, j - 1, self.item(u, "vt"))
            elif not first:
                self.values(pe, n - 1, u - 1, UH - 1, None)
            if j == 0:
                kv = 1 if first else self.item(u - 1, "kv")
                self.turn_values(pe, u, self.item(u, "vt"), self.bank(par, "vt"), kv)
            self.turn_probs(pe, n)

    def tensor(self, pe):
        self.pr.norm_tensor(pe, self)
        pe.wait_ge(self.norm.lo, NT)
        self.project(pe, 0, 0, WBANK[0], QCOL)
        self.project(pe, 0, 1, WBANK[1], 0)
        pe.wait_ge(self.zeroed, self.n_zero)
        self.unit_tensor(pe, 0, 0, first=True)
        self.unit_tensor(pe, 1, 1)
        with pe.Fori(1, UNITS0 // 2 - 1) as k:
            self.unit_tensor(pe, k * 2, 0)
            self.unit_tensor(pe, k * 2 + 1, 1)
        self.unit_tensor(pe, UNITS0 - 2, 0)
        self.unit_tensor(pe, UNITS0 - 1, 1, last=True)
        self.values(pe, UNITS0 * UH - 1, UNITS0 - 1, UH - 1, None)
        for t in range(TB):
            w = self.item(UNITS0 - 1, "q") + t
            self.result(pe, UNITS0 - 1, w, WBANK[w % 2], t)

    n_zero = 9

    def take_q(self, dve, u, bank):
        pr = self.pr
        dve.wait_ge(self.q_hi, u + 1)
        self.nc.vector.scalar_tensor_tensor(out=pr.a_ql[:], in0=pr.ps[:, bank, :], scalar=self.Q_SCALE,
                                            in1=pr.a_qh[:].bitcast(F32), op0=ALU.mult,
                                            op1=ALU.subtract).then_inc(self.taken, 1)

    def take_kv(self, dve, u, bank):
        pr, n = self.pr, UKV * HD0
        dve.wait_ge(self.k_hi, u + 1)
        self.nc.vector.tensor_tensor(pr.a_kl[n:2 * n, :], pr.ps[n:2 * n, bank, :],
                                     pr.a_kh[n:2 * n, :].bitcast(F32), ALU.subtract)
        self.nc.vector.tensor_copy(pr.a_vt[:], pr.ps[:, bank, :]).then_inc(self.taken, 1)

    def value_views(self, bank, kv, dst):
        src = self.pr.ps[:, bank, :].rearrange("p (k n) -> p k n", k=TB)
        return src[:, :, HD0 * kv:HD0 * kv + HD0], dst[:, kv, :, VWIN - P:VWIN - P + HD0]

    def take_vt(self, dve, u, bank):
        pr = self.pr
        dve.wait_ge(self.v_hi, u * UKV + UKV)
        for kv in range(UKV):
            src, lo = self.value_views(bank, kv, pr.a_vl)
            _, hi = self.value_views(bank, kv, pr.a_vh)
            ins = self.nc.vector.tensor_tensor(lo, src, hi.bitcast(F32), ALU.subtract)
        ins.then_inc(self.taken, 1)

    def take_out(self, dve, u):
        pr = self.pr
        dve.wait_ge(self.o_hi, u + 1)
        self.nc.vector.tensor_tensor(pr.a_otl[:], pr.ps[:, OBANK, :], pr.a_oth[:].bitcast(F32),
                                     ALU.subtract).then_inc(self.o_lo, 1)

    def take_result(self, dve, u, w, bank, t):
        dve.wait_ge(self.work, w + 1)
        xm = self.x_tile((u & 3) * TB + t)
        self.nc.vector.tensor_tensor(xm, self.pr.ps[:, bank, :], xm,
                                     ALU.add).then_inc(self.taken, 1)

    def unit_vector(self, dve, u, par, first=False, last=False):
        for j in range(UH):
            n = u * UH + j
            self.maxima(dve, n)
            self.normalise(dve, n)
            if j == 1 and not first:
                for t in range(TB):
                    self.take_result(dve, u - 1, self.item(u, "y", t), self.bank(par, "y", t), t)
            if j == 2 and not last:
                self.take_q(dve, u + 1, self.bank(par, "q"))
            if j == 3 and not last:
                self.take_kv(dve, u + 1, self.bank(par, "kv"))
            if j == 0:
                if not first:
                    self.take_out(dve, u - 1)
                self.take_vt(dve, u, self.bank(par, "vt"))
            self.probs_lo(dve, n)

    def vector(self, dve):
        self.pr.norm_vector(dve, self)
        self.take_q(dve, 0, WBANK[0])
        self.take_kv(dve, 0, WBANK[1])
        self.unit_vector(dve, 0, 0, first=True)
        self.unit_vector(dve, 1, 1)
        with dve.Fori(1, UNITS0 // 2 - 1) as k:
            self.unit_vector(dve, k * 2, 0)
            self.unit_vector(dve, k * 2 + 1, 1)
        self.unit_vector(dve, UNITS0 - 2, 0)
        self.unit_vector(dve, UNITS0 - 1, 1, last=True)
        self.take_out(dve, UNITS0 - 1)
        for t in range(TB):
            w = self.item(UNITS0 - 1, "q") + t
            self.take_result(dve, UNITS0 - 1, w, WBANK[w % 2], t)

    def split_qkv(self, act, u):
        act.wait_ge(self.qkv_in, u * 16 + 16)
        self.nc.scalar.copy(self.pr.a_wh[:], self.pr.a_rawqkv[:]).then_inc(self.qkv_hi, 1)

    def split_wo(self, act, u):
        act.wait_ge(self.wo_in, u * 16 + 16)
        self.nc.scalar.copy(self.pr.a_oh[:], self.pr.a_rawo[:]).then_inc(self.wo_hi, 1)

    def hi_q(self, act, u, w, bank):
        act.wait_ge(self.work, w + 1)
        after(act, self.spread, u * (16 * self.COPIES))
        self.nc.scalar.activation(self.pr.a_qh[:], self.pr.ps[:, bank, :], ACT.Copy,
                                  scale=self.Q_SCALE).then_inc(self.q_hi, 1)

    def hi_kv(self, act, u, w, bank):
        n = UKV * HD0
        act.wait_ge(self.work, w + 1)
        self.nc.scalar.copy(self.pr.a_kh[n:2 * n, :], self.pr.ps[n:2 * n, bank, :]).then_inc(self.k_hi, 1)

    def hi_vt(self, act, w, bank):
        act.wait_ge(self.work, w + 1)
        for kv in range(UKV):
            src, hi = self.value_views(bank, kv, self.pr.a_vh)
            self.nc.scalar.copy(hi, src).then_inc(self.v_hi, 1)

    def hi_out(self, act, u):
        act.wait_ge(self.out, u + 1)
        self.nc.scalar.copy(self.pr.a_oth[:], self.pr.ps[:, OBANK, :]).then_inc(self.o_hi, 1)

    def unit_scalar(self, act, u, par, first=False, last=False, last2=False):
        for j in range(UH):
            n = u * UH + j
            self.exponentials(act, n)
            if j == 2 and not last:
                self.hi_q(act, u + 1, self.item(u, "q"), self.bank(par, "q"))
            if j == 3 and not last:
                self.hi_kv(act, u + 1, self.item(u, "kv"), self.bank(par, "kv"))
            if j == 0:
                if not first:
                    self.hi_out(act, u - 1)
                self.hi_vt(act, self.item(u, "vt"), self.bank(par, "vt"))
            self.probs_hi(act, n)
            if j == 2:
                self.split_wo(act, u)
            if j == 4 and not (last or last2):
                self.split_qkv(act, u + 2)

    def scalar(self, act):
        self.split_qkv(act, 0)
        self.pr.norm_scalar(act, self)
        self.hi_q(act, 0, 0, WBANK[0])
        self.hi_kv(act, 0, 1, WBANK[1])
        self.split_qkv(act, 1)
        self.unit_scalar(act, 0, 0, first=True)
        self.unit_scalar(act, 1, 1)
        with act.Fori(1, UNITS0 // 2 - 1) as k:
            self.unit_scalar(act, k * 2, 0)
            self.unit_scalar(act, k * 2 + 1, 1)
        self.unit_scalar(act, UNITS0 - 2, 0, last2=True)
        self.unit_scalar(act, UNITS0 - 1, 1, last=True)
        self.hi_out(act, UNITS0 - 1)

    def lo_qkv(self, pool, u):
        pr = self.pr
        pool.wait_ge(self.qkv_hi, u + 1)
        self.nc.gpsimd.tensor_tensor(pr.a_wl[:], pr.a_rawqkv[:], pr.a_wh[:].bitcast(F32),
                                     ALU.subtract).then_inc(self.qkv_lo, 1)

    def lo_wo(self, pool, u):
        pr = self.pr
        pool.wait_ge(self.wo_hi, u + 1)
        self.nc.gpsimd.tensor_tensor(pr.a_ol[:], pr.a_rawo[:], pr.a_oh[:].bitcast(F32),
                                     ALU.subtract).then_inc(self.wo_lo, 1)

    def gpsimd(self, pool):
        pr = self.pr
        self.lo_qkv(pool, 0)
        half = P // 2
        self.clear(pool, [pr.a_vh[:].bitcast(F32), pr.a_vl[:].bitcast(F32),
                          pr.a_k2[half:P, 0, 0].bitcast(F32), pr.a_k2[half:P, 1, 0].bitcast(F32),
                          pr.a_k2[0:half, 0, 1].bitcast(F32), pr.a_k2[0:half, 1, 1].bitcast(F32)])
        assert self.cleared == self.n_zero
        self.lo_qkv(pool, 1)
        for u in range(2):
            self.lo_wo(pool, u)
            self.lo_qkv(pool, u + 2)
        with pool.Fori(1, UNITS0 // 2 - 1) as k:
            for s in range(2):
                self.lo_wo(pool, k * 2 + s)
                self.lo_qkv(pool, k * 2 + (s + 2))
        for u in (UNITS0 - 2, UNITS0 - 1):
            self.lo_wo(pool, u)

    def spread_q(self, sp, w, par):
        pr = self.pr
        sp.wait_ge(self.taken, w + 1)
        for h in range(UH):
            for r in range(4):
                at = P // 2 * (h % 2) + HD0 * r
                part = (pr.a_qh, pr.a_ql)[r % 2]
                sp.dma_start(pr.a_q2[at:at + HD0, par, h // 2, :].bitcast(F32),
                             part[HD0 * h:HD0 * h + HD0, :].bitcast(F32)).then_inc(self.spread, 16)

    def spread_k(self, sp, w, par):
        pr = self.pr
        sp.wait_ge(self.taken, w + 1)
        for kv in range(UKV):
            for half in range(2):
                for r in range(4):
                    at = P // 2 * half + HD0 * r
                    src = UKV * HD0 + HD0 * kv
                    part = (pr.a_kh, pr.a_kl)[r // 2]
                    sp.dma_start(pr.a_k2[at:at + HD0, par, half, kv, :].bitcast(F32),
                                 part[src:src + HD0, :].bitcast(F32)).then_inc(self.spread, 16)

    def chunk_sync(self, sp, c, last=False):
        pr = self.pr
        for b in range(BATCH):
            u = c * BATCH + b
            if not (last and b + 2 >= BATCH):
                sp.wait_ge(self.qkv_lo, u + 2)
                rows = c * P + (P if b + 2 >= BATCH else 0)
                sp.dma_start(pr.a_rawqkv[:], pr.io["at0_qkv"][ds(rows, P), :]).then_inc(self.qkv_in, 16)
            if not (last and b + 1 >= BATCH):
                sp.wait_ge(self.wo_lo, u + 1)
                rows = c * P + (P if b + 1 >= BATCH else 0)
                sp.dma_start(pr.a_rawo[:], pr.io["at0_o"][ds(rows, P), :]).then_inc(self.wo_in, 16)
                self.spread_q(sp, self.item(u, "q"), 1 - b % 2)
                self.spread_k(sp, self.item(u, "kv"), 1 - b % 2)

    def sync(self, sp):
        pr = self.pr
        if self.prev is not None:
            sp.wait_ge(self.prev.x_new, self.prev.x_new_total)
        sp.dma_start(pr.a_rawqkv[:], pr.io["at0_qkv"][0:P, :]).then_inc(self.qkv_in, 16)
        sp.dma_start(pr.a_rawo[:], pr.io["at0_o"][0:P, :]).then_inc(self.wo_in, 16)
        sp.wait_ge(self.qkv_lo, 1)
        sp.dma_start(pr.a_rawqkv[:], pr.io["at0_qkv"][0:P, :]).then_inc(self.qkv_in, 16)
        sp.wait_ge(self.zeroed, self.n_zero)
        self.spread_q(sp, 0, 0)
        self.spread_k(sp, 1, 0)
        self.chunk_sync(sp, 0)
        with sp.Fori(1, C - 1) as c:
            self.chunk_sync(sp, c)
        self.chunk_sync(sp, C - 1, last=True)


class RopeHeads(Heads):

    x_new_total = UNITS1 * 11

    def __init__(self, pr, tag):
        super().__init__(pr, tag)
        sem = pr.sem
        self.tables_in = sem(f"{tag}_tables_in")
        self.w_in = sem(f"{tag}_w_in")
        self.w_hi = sem(f"{tag}_w_hi")
        self.w_lo = sem(f"{tag}_w_lo")
        self.swap = sem(f"{tag}_swap")
        self.sine = sem(f"{tag}_sine")
        self.turned = sem(f"{tag}_turned")
        self.t_hi = sem(f"{tag}_t_hi")
        self.t_lo = sem(f"{tag}_t_lo")
        self.v_hi = sem(f"{tag}_v_hi")

    AHEAD = {"k": 0, "v": 1, "q0": 2, "q1": 3}
    ORDER = {"q0": 0, "k": 1, "vt": 2, "q1": 3, "y": 4, "q2": 8, "v": 9, "q3": 10}
    ORDER_FIRST = {"q0": 0, "k": 1, "vt": 2, "q1": 3, "q2": 4, "v": 5, "q3": 6}
    ORDER_LAST = {"q0": 0, "vt": 1, "q1": 2, "y": 3, "end": 7}

    def item(self, u, kind, j=0):
        if isinstance(u, int) and u == 0:
            return len(self.AHEAD) + self.ORDER_FIRST[kind]
        order = self.ORDER_LAST if isinstance(u, int) and u == UNITS1 - 1 else self.ORDER
        return u * 11 + (order[kind] + j)

    def bank(self, u, par, kind, j=0):
        if isinstance(u, int):
            return WBANK[self.item(u, kind, j) % 2]
        return WBANK[(par * 11 + self.ORDER[kind] + j) % 2]

    @staticmethod
    def rotation(u, kind):
        return u * 5 + (3 + {"q0": 0, "k": 1, "q1": 2, "q2": 3, "q3": 4}[kind])

    def project(self, pe, w, bank, piece, need, batch):
        pr = self.pr
        pe.wait_ge(self.w_lo, need)
        after(pe, self.taken, w - 1)
        tok = slice(SEQ * batch, SEQ * batch + SEQ)
        for c in range(C):
            for a, wt, x in ((0, pr.r_wh, pr.xh), (1, pr.r_wh, pr.xl), (2, pr.r_wl, pr.xh)):
                last = self.nc.tensor.matmul(pr.ps[:, bank, :], wt[:, piece, P * c:P * c + P], x[:, c, tok],
                                             start=(c == 0 and a == 0), stop=(c == C - 1 and a == 2))
        last.then_inc(self.work, 1)

    def turn_values(self, pe, w, bank, w_v):
        pr = self.pr
        pe.wait_ge(self.taken, w_v + 1)
        after(pe, self.taken, w - 1)
        for k in range(TB):
            last = self.nc.tensor.transpose(pr.ps[:, bank, P * k:P * k + P], pr.r_vt[:, P * k:P * k + P],
                                            pr.ident[:])
        last.then_inc(self.work, 1)

    def results(self, pe, u, need, items):
        pr = self.pr
        pe.wait_ge(self.o_lo, u * R1 + R1)
        pe.wait_ge(self.w_lo, need)
        for t, (w, bank) in enumerate(items):
            after(pe, self.taken, w - 1)
            tok = slice(P * t, P * t + P)
            for h in range(R1):
                o = PIECES - R1 + h
                for a, x, wt in ((0, pr.r_oth, pr.r_wh), (1, pr.r_oth, pr.r_wl), (2, pr.r_otl, pr.r_wh)):
                    last = self.nc.tensor.matmul(pr.ps[:, bank, :], x[:, h, tok], wt[:, o, :],
                                                 start=(h == 0 and a == 0), stop=(h == R1 - 1 and a == 2))
            last.then_inc(self.work, 1)

    def output(self, pe, n):
        pr = self.pr
        after(pe, self.o_lo, n)
        self.attend(pe, n, lambda k: pr.r_vh[:, k, :], lambda k: pr.r_vl[:, k, :],
                    first=True, end=True).then_inc(self.out, 1)

    def group_tensor(self, pe, g, first=False, last=False):
        pr = self.pr
        for b in range(BATCH):
            u, par = g * BATCH + b, b % 2
            u_first, u_last = first and b == 0, last and b == BATCH - 1
            nb, ng = (b + 1) % BATCH, g + (b + 1) // BATCH
            for j in range(R1):
                n = u * R1 + j
                pe.wait_ge(self.t_lo, u * 5 + (2, 3, 4, 5 if u_last else 6)[j])
                self.scores(pe, n, [(pr.r_qh[:, j % 2, :], pr.r_kh[:, par, :]),
                                    (pr.r_qh[:, j % 2, :], pr.r_kl[:, par, :]),
                                    (pr.r_ql[:, j % 2, :], pr.r_kh[:, par, :])])
                q = (j + 2) % R1
                if not (u_last and j >= 2):
                    self.project(pe, self.item(u, f"q{j}"), self.bank(u, par, f"q{j}"), 2 + q,
                                 (g if j < 2 else ng) * PIECES + (3 + q), b if j < 2 else nb)
                if j == 0 and not u_last:
                    self.project(pe, self.item(u, "k"), self.bank(u, par, "k"), 0, ng * PIECES + 1, nb)
                if j == 1 and not u_first:
                    self.results(pe, u - 1, (g if b == 0 else g + 1) * PIECES,
                                 [(self.item(u, "y", t), self.bank(u, par, "y", t)) for t in range(TB)])
                if j == 2 and not u_last:
                    self.project(pe, self.item(u, "v"), self.bank(u, par, "v"), 1, ng * PIECES + 2, nb)
                if j == 1:
                    pe.wait_ge(self.taken, self.item(u, "vt") + 1)
                if not (u_first and j == 0):
                    self.output(pe, n - 1)
                if j == 0:
                    self.turn_values(pe, self.item(u, "vt"), self.bank(u, par, "vt"),
                                     self.AHEAD["v"] if u_first else self.item(u - 1, "v"))
                self.turn_probs(pe, n)

    def tensor(self, pe):
        self.pr.norm_tensor(pe, self)
        pe.wait_ge(self.norm.lo, NT)
        for kind, piece in (("k", 0), ("v", 1), ("q0", 2), ("q1", 3)):
            w = self.AHEAD[kind]
            self.project(pe, w, WBANK[w % 2], piece, piece + 1, 0)
        pe.wait_ge(self.zeroed, self.n_zero)
        self.group_tensor(pe, 0, first=True)
        with pe.Fori(1, G1 - 1) as g:
            self.group_tensor(pe, g)
        self.group_tensor(pe, G1 - 1, last=True)
        self.output(pe, UNITS1 * R1 - 1)
        u = UNITS1 - 1
        self.results(pe, u, G1 * PIECES, [(self.item(u, "end", t), self.bank(u, 1, "end", t)) for t in range(TB)])

    n_zero = 3

    def rotate(self, dve, r, bank):
        pr, nc = self.pr, self.nc
        dve.wait_ge(self.swap, r + 1)
        after(dve, self.t_lo, r)
        nc.vector.tensor_tensor(pr.r_t[:], pr.ps[:, bank, :], pr.r_cos[:], ALU.mult).then_inc(self.taken, 1)
        nc.vector.tensor_tensor(pr.r_sw[:], pr.r_sw[:], pr.r_sin[:], ALU.mult).then_inc(self.sine, 1)

    def take_v(self, dve, w, bank):
        dve.wait_ge(self.work, w + 1)
        self.nc.vector.tensor_copy(self.pr.r_vt[:], self.pr.ps[:, bank, :]).then_inc(self.taken, 1)

    def take_vt(self, dve, u, bank):
        pr = self.pr
        dve.wait_ge(self.v_hi, u + 1)
        self.nc.vector.tensor_tensor(pr.r_vl[:], pr.ps[:, bank, :].rearrange("p (k d) -> p k d", k=TB),
                                     pr.r_vh[:].bitcast(F32), ALU.subtract).then_inc(self.taken, 1)

    def take_out(self, dve, n, j):
        pr = self.pr
        dve.wait_ge(self.o_hi, n + 1)
        self.nc.vector.tensor_tensor(pr.r_otl[:, j, :], pr.ps[:, OBANK, :], pr.r_oth[:, j, :].bitcast(F32),
                                     ALU.subtract).then_inc(self.o_lo, 1)

    def take_result(self, dve, m, w, bank):
        dve.wait_ge(self.work, w + 1)
        xm = self.pr.x[:, m, :]
        self.nc.vector.tensor_tensor(xm, self.pr.ps[:, bank, :], xm, ALU.add).then_inc(self.taken, 1)

    def group_vector(self, dve, g, first=False, last=False):
        for b in range(BATCH):
            u, par = g * BATCH + b, b % 2
            u_first, u_last = first and b == 0, last and b == BATCH - 1
            for j in range(R1):
                n = u * R1 + j
                self.maxima(dve, n)
                self.normalise(dve, n)
                if not (u_last and j >= 2):
                    self.rotate(dve, self.rotation(u, f"q{j}") - (1 if u_last and j else 0),
                                self.bank(u, par, f"q{j}"))
                if j == 0 and not u_last:
                    self.rotate(dve, self.rotation(u, "k"), self.bank(u, par, "k"))
                if j == 1 and not u_first:
                    for t in range(TB):
                        self.take_result(dve, TB * ((b - 1) % BATCH) + t, self.item(u, "y", t),
                                         self.bank(u, par, "y", t))
                if j == 2 and not u_last:
                    self.take_v(dve, self.item(u, "v"), self.bank(u, par, "v"))
                if not (u_first and j == 0):
                    self.take_out(dve, n - 1, (j - 1) % R1)
                if j == 0:
                    self.take_vt(dve, u, self.bank(u, par, "vt"))
                self.probs_lo(dve, n)

    def vector(self, dve):
        self.pr.norm_vector(dve, self)
        dve.wait_ge(self.tables_in, 2 * 16)
        self.rotate(dve, 0, WBANK[self.AHEAD["k"] % 2])
        self.take_v(dve, self.AHEAD["v"], WBANK[self.AHEAD["v"] % 2])
        self.rotate(dve, 1, WBANK[self.AHEAD["q0"] % 2])
        self.rotate(dve, 2, WBANK[self.AHEAD["q1"] % 2])
        self.group_vector(dve, 0, first=True)
        with dve.Fori(1, G1 - 1) as g:
            self.group_vector(dve, g)
        self.group_vector(dve, G1 - 1, last=True)
        self.take_out(dve, UNITS1 * R1 - 1, R1 - 1)
        u = UNITS1 - 1
        for t in range(TB):
            self.take_result(dve, TB * (BATCH - 1) + t, self.item(u, "end", t), self.bank(u, 1, "end", t))

    def split(self, act, p, slot):
        act.wait_ge(self.w_in, p * 16 + 16)
        self.nc.scalar.copy(self.pr.r_wh[:, slot, :], self.pr.r_raw[:]).then_inc(self.w_hi, 1)

    def swap_halves(self, act, r, w, bank):
        pr, half = self.pr, P // 2
        act.wait_ge(self.work, w + 1)
        after(act, self.turned, r)
        self.nc.scalar.copy(pr.r_sw[0:half, :], pr.ps[half:P, bank, :])
        self.nc.scalar.copy(pr.r_sw[half:P, :], pr.ps[0:half, bank, :]).then_inc(self.swap, 1)

    def turned_hi(self, act, r, part):
        act.wait_ge(self.turned, r + 1)
        self.nc.scalar.copy(part, self.pr.r_t[:]).then_inc(self.t_hi, 1)

    def hi_vt(self, act, w, bank):
        pr = self.pr
        act.wait_ge(self.work, w + 1)
        self.nc.scalar.copy(pr.r_vh[:], pr.ps[:, bank, :].rearrange("p (k d) -> p k d", k=TB)
                            ).then_inc(self.v_hi, 1)

    def hi_out(self, act, n, j):
        act.wait_ge(self.out, n + 1)
        self.nc.scalar.copy(self.pr.r_oth[:, j, :], self.pr.ps[:, OBANK, :]).then_inc(self.o_hi, 1)

    SPLITS = {1: 6, 2: 7, 3: 8, 4: 9, 9: 10, 11: 11, 12: 12, 13: 13, 14: 14, 15: 15}

    def group_scalar(self, act, g, first=False, last=False):
        pr = self.pr
        for b in range(BATCH):
            u, par = g * BATCH + b, b % 2
            u_first, u_last = first and b == 0, last and b == BATCH - 1
            for j in range(R1):
                n = u * R1 + j
                self.exponentials(act, n)
                more = not (u_last and j >= 2)
                if more:
                    r = self.rotation(u, f"q{j}") - (1 if u_last and j else 0)
                    self.swap_halves(act, r, self.item(u, f"q{j}"), self.bank(u, par, f"q{j}"))
                if j == 0:
                    self.turned_hi(act, r, pr.r_qh[:, 0, :])
                if j == 0 and not u_last:
                    self.swap_halves(act, self.rotation(u, "k"), self.item(u, "k"), self.bank(u, par, "k"))
                if not (u_first and j == 0):
                    self.hi_out(act, n - 1, (j - 1) % R1)
                if j == 0:
                    self.hi_vt(act, self.item(u, "vt"), self.bank(u, par, "vt"))
                self.probs_hi(act, n)
                if j == 0 and not u_last:
                    self.turned_hi(act, self.rotation(u, "k"), pr.r_kh[:, 1 - par, :])
                if j > 0 and more:
                    self.turned_hi(act, r, pr.r_qh[:, j % 2, :])
                piece = self.SPLITS.get(R1 * b + j)
                if piece is not None and not (last and piece >= PIECES):
                    self.split(act, g * PIECES + piece, piece % PIECES)

    def scalar(self, act):
        pr = self.pr
        for piece in range(2):
            self.split(act, piece, piece)
        pr.norm_scalar(act, self)
        for piece in range(2, 4):
            self.split(act, piece, piece)
        for r, (kind, part) in enumerate((("k", pr.r_kh), ("q0", pr.r_qh), ("q1", pr.r_qh))):
            w = self.AHEAD[kind]
            self.swap_halves(act, r, w, WBANK[w % 2])
            self.turned_hi(act, r, part[:, 1 if kind == "q1" else 0, :])
        for piece in range(4, 6):
            self.split(act, piece, piece)
        self.group_scalar(act, 0, first=True)
        with act.Fori(1, G1 - 1) as g:
            self.group_scalar(act, g)
        self.group_scalar(act, G1 - 1, last=True)
        self.hi_out(act, UNITS1 * R1 - 1, R1 - 1)

    def split_lo(self, pool, p, slot):
        pr = self.pr
        pool.wait_ge(self.w_hi, p + 1)
        self.nc.gpsimd.tensor_tensor(pr.r_wl[:, slot, :], pr.r_raw[:], pr.r_wh[:, slot, :].bitcast(F32),
                                     ALU.subtract).then_inc(self.w_lo, 1)

    def rotated(self, pool, r, hi, lo):
        pr = self.pr
        pool.wait_ge(self.sine, r + 1)
        self.nc.gpsimd.tensor_tensor(pr.r_t[:], pr.r_t[:], pr.r_sw[:], ALU.add).then_inc(self.turned, 1)
        pool.wait_ge(self.t_hi, r + 1)
        self.nc.gpsimd.tensor_tensor(lo, pr.r_t[:], hi.bitcast(F32), ALU.subtract).then_inc(self.t_lo, 1)

    def group_gpsimd(self, pool, g, last=False):
        pr = self.pr
        for b in range(BATCH):
            u, par = g * BATCH + b, b % 2
            u_last = last and b == BATCH - 1
            for j in range(R1):
                if not (u_last and j >= 2):
                    self.rotated(pool, self.rotation(u, f"q{j}") - (1 if u_last and j else 0),
                                 pr.r_qh[:, j % 2, :], pr.r_ql[:, j % 2, :])
                if j == 0 and not u_last:
                    self.rotated(pool, self.rotation(u, "k"), pr.r_kh[:, 1 - par, :], pr.r_kl[:, 1 - par, :])
                piece = self.SPLITS.get(R1 * b + j)
                if piece is not None and not (last and piece >= PIECES):
                    self.split_lo(pool, g * PIECES + piece, piece % PIECES)

    def gpsimd(self, pool):
        pr = self.pr
        for piece in range(2):
            self.split_lo(pool, piece, piece)
        self.clear(pool, [])
        assert self.cleared == self.n_zero
        for piece in range(2, 4):
            self.split_lo(pool, piece, piece)
        self.rotated(pool, 0, pr.r_kh[:, 0, :], pr.r_kl[:, 0, :])
        for r, s in ((1, 0), (2, 1)):
            self.rotated(pool, r, pr.r_qh[:, s, :], pr.r_ql[:, s, :])
        for piece in range(4, 6):
            self.split_lo(pool, piece, piece)
        self.group_gpsimd(pool, 0)
        with pool.Fori(1, G1 - 1) as g:
            self.group_gpsimd(pool, g)
        self.group_gpsimd(pool, G1 - 1, last=True)

    def load_piece(self, sp, p, rows):
        pr = self.pr
        after(sp, self.w_lo, p)
        sp.dma_start(pr.r_raw[:], pr.io["at1_w"][ds(rows, P), :]).then_inc(self.w_in, 16)

    def sync(self, sp):
        pr = self.pr
        if self.prev is not None:
            sp.wait_ge(self.prev.x_new, self.prev.x_new_total)
        self.load_piece(sp, 0, 0)
        sp.dma_start(pr.r_cos[:], pr.io["at1_cos"]).then_inc(self.tables_in, 16)
        sp.dma_start(pr.r_sin[:], pr.io["at1_sin"]).then_inc(self.tables_in, 16)
        for p in range(1, 6 + PIECES):
            self.load_piece(sp, p, p * P)
        with sp.Fori(1, G1 - 1) as g:
            for k in range(6, 6 + PIECES):
                self.load_piece(sp, g * PIECES + k, g * (PIECES * P) + k * P)
        for k in range(6, PIECES):
            p = (G1 - 1) * PIECES + k
            self.load_piece(sp, p, p * P)


def rope_tables():
    inv = 1.0 / 500000.0 ** (np.arange(0, HD1, 2, dtype=np.float64) / HD1)
    wavelen = 2.0 * np.pi / inv
    low_wl, high_wl = 1024 / 1.0, 1024 / 4.0
    smooth = (1024 / wavelen - 1.0) / (4.0 - 1.0)
    scaled = np.where(wavelen > low_wl, inv / 8.0, inv)
    mid = (wavelen <= low_wl) & (wavelen >= high_wl)
    scaled = np.where(mid, (1 - smooth) * inv / 8.0 + smooth * inv, scaled).astype(np.float32)
    freqs = np.arange(SEQ, dtype=np.float32)[:, None] * scaled[None, :]
    emb = np.concatenate([freqs, freqs], axis=-1)
    return np.cos(emb).T, np.sin(emb).T


def build(nc, io):
    Program(nc, io)


def kernel(**inputs):
    import concourse.bacc as bacc
    from concourse.bass_utils import run_bass_kernel_spmd

    a = {k: np.asarray(v) for k, v in inputs.items()}
    arrays = layout(a)
    nc = bacc.Bacc("TRN2", target_bir_lowering=False, num_devices=1)
    io = {k: nc.dram_tensor(f"in_{k}", v.shape, mybir.dt.from_np(v.dtype), kind="ExternalInput").ap()
          for k, v in arrays.items()}
    io["out"] = nc.dram_tensor("out", (TOK, D), F32, kind="ExternalOutput").ap()
    build(nc, io)
    r = run_bass_kernel_spmd(nc, [{f"in_{k}": v for k, v in arrays.items()}], core_ids=[0])
    return r.results[0]["out"].reshape(BATCH, SEQ, D)


def layout(a):
    def rows(w):
        return w.reshape(P, C, -1)

    out = {"x": a["L0_attn_x"].reshape(TOK, D)}
    gate, up = rows(a["L0_ffn_w_gate"].T), rows(a["L0_ffn_w_up"].T)
    down = a["L0_ffn_w_down"].T
    n = (IT - 1) * P
    gu = np.concatenate([w[:, :, :n].reshape(P, C, IT - 1, P).transpose(2, 0, 1, 3) for w in (gate, up)], 2)
    b = np.stack([a["L0_ffn_b_gate"], a["L0_ffn_b_up"]], 1)
    out["ffn_w"] = np.concatenate([gu.reshape(IT - 1, P, 2 * C * P), down[:n].reshape(IT - 1, P, D),
                                   b[:n].reshape(IT - 1, P, 2)], 2)
    out["ffn_gu_last"] = np.concatenate([gate[:, :, n:], up[:, :, n:]], 1)
    out["ffn_d_last"] = np.concatenate([down[n:], b[n:]], 1)
    out["ffn_bd"] = a["L0_ffn_b_down"]
    out["deq_q"] = a["L1_ffn_qweight"].T.reshape(P, 3, D)
    out["deq_zp"] = a["L1_ffn_weight_zero_point"].reshape(D)
    out["deq_sc"] = a["L1_ffn_weight_scale"].reshape(D)
    out["deq_b"] = a["L1_ffn_bias"]
    q, k, v = (rows(a[f"L0_attn_w{n}"]).reshape(P, C, C, -1).transpose(2, 0, 1, 3) for n in "qkv")
    out["at0_qkv"] = np.concatenate([v, k, q], 3).reshape(C * P, QKV0_W)
    out["at0_o"] = a["L0_attn_wo"]
    q, k, v = (a[f"L1_attn_w{n}"].reshape(P, C, -1, HD1).transpose(2, 0, 1, 3).reshape(-1, P, C * HD1) for n in "qkv")
    o = a["L1_attn_wo"].reshape(G1, R1, P, D)
    q = q.reshape(G1, R1, P, C * HD1)
    out["at1_w"] = np.concatenate([k[:, None], v[:, None], q, o], 1).reshape(G1 * PIECES * P, C * HD1)
    cos, sin = (t.astype(np.float64) * HD1 ** -0.25 for t in rope_tables())
    sin[:HD1 // 2] *= -1
    out["at1_cos"], out["at1_sin"] = cos.astype(np.float32), sin.astype(np.float32)
    return {k: np.ascontiguousarray(v) for k, v in out.items()}
```

```python
from contextlib import ExitStack

import numpy as np

import concourse.bass as bass
from concourse import mybir

F32 = mybir.dt.float32
F32R = mybir.dt.float32r
BF16 = mybir.dt.bfloat16
I32 = mybir.dt.int32
ALU = mybir.AluOpType
ACT = mybir.ActivationFunctionType
AX = mybir.AxisListType
ds = bass.ds

P = 128
BATCH, SEQ, D = 4, 512, 512
TOK = BATCH * SEQ
NT = TOK // P
TB = SEQ // P
C = D // P
EPS = 1e-5
RSQRT_MAGIC = float(0x5F3759DF)

INTER = 1376
IT = 11
I_LAST = INTER - (IT - 1) * P
FFN_M = 2 * C * P + D
FFN_W = FFN_M + 2

H0, HD0 = 32, 16
KV0 = 8
UH = P // HD0
UKV = UH * KV0 // H0
UNITS0 = H0 // UH * BATCH
QCOL = 2 * UKV * HD0
QKV0_W = C * (QCOL + P)
VWIN = 2 * P - HD0

HD1 = 128
G1, R1 = 8, 4
UNITS1 = G1 * BATCH
PIECES = 2 + 2 * R1

NEG = -1e30
QORDER = (3, 2, 0, 1)
GROUPS = ((3,), (2,), (0, 1))
SBANK = {3: (2, 0), 2: (1, 0), 0: (0, 0), 1: (0, 256)}
SWIDE = {0: 256, 1: 256, 2: 384, 3: 512}
POFF = {0: 0, 1: 128, 2: 384, 3: 768}
PWIDE = 1280
TBANK = {"A": 3, "B": 4, "C": 0}
OBANK = 6
WBANK = (5, 7)


def after(eng, sem, count):
    if not (isinstance(count, int) and count <= 0):
        eng.wait_ge(sem, count)


class Norm:

    def __init__(self, sem, tag):
        self.chain = sem(f"{tag}_stat")
        self.steps = 0
        self.normed = sem(f"{tag}_normed")
        self.turned = sem(f"{tag}_turned")
        self.hi = sem(f"{tag}_hi")
        self.lo = sem(f"{tag}_lo")
        self.biased = sem(f"{tag}_biased")

    def step(self, instruction):
        self.steps += 1
        instruction.then_inc(self.chain, 1)


class Program:
    def __init__(self, nc, io):
        self.nc, self.io = nc, io
        self.ctx = ExitStack()
        with self.ctx:
            self.place()
            self.run()

    def place(self):
        nc, keep = self.nc, self.ctx

        def sem(name):
            return keep.enter_context(nc.semaphore(name))

        def tensor(stack, name, shape, dt=F32):
            return stack.enter_context(nc.sbuf_tensor(name, shape, dt))

        self.sem = sem
        self.ps = keep.enter_context(nc.psum_tensor("ps", [P, 8, 512], F32))
        self.x = tensor(keep, "x", [P, NT, D])
        self.xh = tensor(keep, "xh", [P, C, TOK], F32R)
        self.xl = tensor(keep, "xl", [P, C, TOK], F32R)
        self.n_st = tensor(keep, "n_st", [P, NT, 6])
        self.n_mv = tensor(keep, "n_mv", [P, NT, 2])
        self.n_v = tensor(keep, "n_v", [P, NT])
        self.n_y = tensor(keep, "n_y", [P, NT])
        self.n_t = tensor(keep, "n_t", [P, NT])
        self.ident = tensor(keep, "ident", [P, P])
        self.identb = tensor(keep, "identb", [P, P], BF16)
        self.maskb = tensor(keep, "maskb", [P, P], BF16)

        with ExitStack() as s:
            self.n_xn = tensor(s, "n_xn", [P, TB, D])
            self.hb = tensor(s, "hb", [P, D])
            self.hbraw = tensor(s, "hbraw", [P, D])
            with ExitStack() as f:
                self.f_raw = tensor(f, "f_raw", [P, 2, FFN_W])
                self.f_hi = tensor(f, "f_hi", [P, 2, FFN_M], F32R)
                self.f_lo = tensor(f, "f_lo", [P, 2, FFN_M], F32R)
                self.f_bias = tensor(f, "f_bias", [P, 2, 2])
                self.f_zero = tensor(f, "f_zero", [P, D + 2])
                self.f_silu = tensor(f, "f_silu", [P, 2, SEQ])
                self.f_h = tensor(f, "f_h", [P, 2, SEQ])
                self.f_hh = tensor(f, "f_hh", [P, 2, SEQ], F32R)
                self.f_hl = tensor(f, "f_hl", [P, 2, SEQ], F32R)
            with ExitStack() as f:
                self.d_q = tensor(f, "d_q", [P, 3, D], I32)
                self.d_u = tensor(f, "d_u", [P, C, D], I32)
                self.d_zp = tensor(f, "d_zp", [P, D])
                self.d_sc = tensor(f, "d_sc", [P, D])
                self.d_w = tensor(f, "d_w", [P, C, D])
                self.d_wh = tensor(f, "d_wh", [P, C, D], F32R)
                self.d_wl = tensor(f, "d_wl", [P, C, D], F32R)
        with ExitStack() as s:
            self.p = tensor(s, "p", [P, PWIDE])
            self.pth = tensor(s, "pth", [P, TB, SEQ], F32R)
            self.ptl = tensor(s, "ptl", [P, TB, SEQ], F32R)
            self.nmax = tensor(s, "nmax", [P, TB])
            self.psum_ = tensor(s, "psums", [P, TB])
            self.rsum = tensor(s, "rsum", [P, TB])
            with ExitStack() as f:
                self.a_pth = tensor(f, "a_pth", [P, TB, SEQ], F32R)
                self.a_ptl = tensor(f, "a_ptl", [P, TB, SEQ], F32R)
                self.a_raw = tensor(f, "a_raw", [P, QKV0_W])
                self.a_wh = tensor(f, "a_wh", [P, QKV0_W], F32R)
                self.a_wl = tensor(f, "a_wl", [P, QKV0_W], F32R)
                self.a_oh = tensor(f, "a_oh", [P, D], F32R)
                self.a_ol = tensor(f, "a_ol", [P, D], F32R)
                self.a_qh = tensor(f, "a_qh", [P, SEQ], F32R)
                self.a_ql = tensor(f, "a_ql", [P, SEQ], F32R)
                self.a_kh = tensor(f, "a_kh", [P, SEQ], F32R)
                self.a_kl = tensor(f, "a_kl", [P, SEQ], F32R)
                self.a_q2 = tensor(f, "a_q2", [P, 2, UH // 2, SEQ], F32R)
                self.a_k2 = tensor(f, "a_k2", [P, 2, 2, UKV, SEQ], F32R)
                self.a_vh = tensor(f, "a_vh", [P, UKV, TB, VWIN], F32R)
                self.a_vl = tensor(f, "a_vl", [P, UKV, TB, VWIN], F32R)
                self.a_oth = tensor(f, "a_oth", [P, SEQ], F32R)
                self.a_otl = tensor(f, "a_otl", [P, SEQ], F32R)
            with ExitStack() as f:
                self.r_raw = tensor(f, "r_raw", [P, 512])
                self.r_wh = tensor(f, "r_wh", [P, PIECES, 512], F32R)
                self.r_wl = tensor(f, "r_wl", [P, PIECES, 512], F32R)
                self.r_cos = tensor(f, "r_cos", [P, SEQ])
                self.r_sin = tensor(f, "r_sin", [P, SEQ])
                self.r_t = tensor(f, "r_t", [P, SEQ])
                self.r_sw = tensor(f, "r_sw", [P, SEQ])
                self.r_qh = tensor(f, "r_qh", [P, 2, SEQ], F32R)
                self.r_ql = tensor(f, "r_ql", [P, 2, SEQ], F32R)
                self.r_kh = tensor(f, "r_kh", [P, 2, SEQ], F32R)
                self.r_kl = tensor(f, "r_kl", [P, 2, SEQ], F32R)
                self.r_vt = tensor(f, "r_vt", [P, SEQ])
                self.r_vh = tensor(f, "r_vh", [P, TB, HD1], F32R)
                self.r_vl = tensor(f, "r_vl", [P, TB, HD1], F32R)
                self.r_oth = tensor(f, "r_oth", [P, R1, SEQ], F32R)
                self.r_otl = tensor(f, "r_otl", [P, R1, SEQ], F32R)

        self.x_in = [sem(f"x_in{b}") for b in range(BATCH)]
        self.consts = sem("consts")
        self.x_out = sem("x_out")

    def run(self):
        io = self.io
        gated = dict(w=io["ffn_w"], w_gu_last=io["ffn_gu_last"], w_d_last=io["ffn_d_last"],
                     out_bias=io["ffn_bd"])
        deq = dict(q=io["deq_q"], zp=io["deq_zp"], sc=io["deq_sc"], out_bias=io["deq_b"])
        stages = [
            GatedFfn(self, "ffn0a", **gated), SmallHeads(self, "attn0"), GatedFfn(self, "ffn0b", **gated),
            DequantFfn(self, "ffn1a", **deq), RopeHeads(self, "attn1"), DequantFfn(self, "ffn1b", **deq),
        ]
        for prev, s, following in zip([None] + stages, stages, stages[1:] + [None]):
            s.prev, s.next = prev, following
        last = stages[-1]
        nc = self.nc
        block = self.ctx.enter_context(nc.Block())

        @block.sync
        def _(sp):
            for b in range(BATCH):
                sp.dma_start(self.x[:, TB * b:TB * b + TB, :],
                             io["x"][SEQ * b:SEQ * b + SEQ, :].rearrange("(t p) d -> p t d", p=P)
                             ).then_inc(self.x_in[b], 16)
            for s in stages:
                s.sync(sp)
            for m in range(NT):
                sp.wait_ge(last.x_new, last.tile_ready(m))
                sp.dma_start(io["out"][P * m:P * m + P, :], self.x[:, m, :]).then_inc(self.x_out, 16)
            sp.wait_ge(self.x_out, 16 * NT)

        @block.gpsimd
        def _(pool):
            nc.gpsimd.memset(self.ident[:], 0.0).then_inc(self.consts, 1)
            nc.gpsimd.memset(self.maskb[:], 0.0).then_inc(self.consts, 1)
            pool.wait_ge(self.consts, 2)
            nc.gpsimd.affine_select(out=self.ident[:], in_=self.ident[:], compare_op=ALU.not_equal,
                                    fill=1.0, base=0, pattern=[[-1, P]],
                                    channel_multiplier=1).then_inc(self.consts, 1)
            nc.gpsimd.affine_select(out=self.maskb[:], in_=self.maskb[:], compare_op=ALU.is_ge,
                                    fill=NEG, base=0, pattern=[[-1, P]],
                                    channel_multiplier=1).then_inc(self.consts, 1)
            pool.wait_ge(self.consts, 4)
            nc.gpsimd.tensor_copy(self.identb[:], self.ident[:]).then_inc(self.consts, 1)
            for s in stages:
                s.gpsimd(pool)

        @block.scalar
        def _(act):
            for s in stages:
                s.scalar(act)

        @block.vector
        def _(dve):
            for s in stages:
                s.vector(dve)

        @block.tensor
        def _(pe):
            pe.wait_ge(self.consts, 5)
            for s in stages:
                s.tensor(pe)

    def batch_stats(self, dve, s, b):
        if s is None:
            return
        nc, nm = self.nc, s.norm
        for m in range(TB * b, TB * b + TB):
            nm.step(nc.vector.bn_stats(self.n_st[:, m, :], self.x[:, m, :]))
        for m in range(TB * b, TB * b + TB):
            dve.wait_ge(nm.chain, nm.steps - TB + 1)
            nm.step(nc.vector.bn_aggr(self.n_mv[:, m, :], self.n_st[:, m, :]))

    def inverse_deviation(self, dve, s, tiles):
        nc, nm = self.nc, s.norm
        v, y, t = self.n_v[:, tiles], self.n_y[:, tiles], self.n_t[:, tiles]
        dve.wait_ge(nm.chain, nm.steps)
        nm.step(nc.vector.tensor_scalar(v, self.n_mv[:, tiles, 1], EPS, None, ALU.add))
        dve.wait_ge(nm.chain, nm.steps)
        nm.step(nc.vector.tensor_scalar(y.bitcast(I32), v.bitcast(I32), -0.5, RSQRT_MAGIC,
                                        ALU.mult, ALU.add))
        for _ in range(4):
            dve.wait_ge(nm.chain, nm.steps)
            nm.step(nc.vector.scalar_tensor_tensor(out=t, in0=y, scalar=-0.5, in1=y, op0=ALU.mult,
                                                   op1=ALU.mult))
            dve.wait_ge(nm.chain, nm.steps)
            nm.step(nc.vector.tensor_tensor(t, t, v, ALU.mult))
            dve.wait_ge(nm.chain, nm.steps)
            nm.step(nc.vector.scalar_tensor_tensor(out=y, in0=t, scalar=1.5, in1=y, op0=ALU.add,
                                                   op1=ALU.mult))
        dve.wait_ge(nm.chain, nm.steps)

    def norm_vector(self, dve, s, hook=None, meanwhile=None):
        nc, nm = self.nc, s.norm

        def normalise(m):
            after(dve, nm.turned, m - TB + 1)
            if s.prev is None and m % TB == 0:
                dve.wait_ge(self.x_in[m // TB], 16)
                self.batch_stats(dve, s, m // TB)
                self.inverse_deviation(dve, s, slice(m, m + TB))
            nc.vector.tensor_scalar(self.n_xn[:, m % TB, :], self.x[:, m, :], self.n_mv[:, m, 0:1],
                                    self.n_y[:, m:m + 1], ALU.subtract, ALU.mult).then_inc(nm.normed, 1)

        if s.prev is not None:
            dve.wait_ge(s.prev.x_new, s.prev.x_new_total)
            self.inverse_deviation(dve, s, slice(0, NT))
        for m in range(TB):
            normalise(m)
        if meanwhile is not None:
            meanwhile()
        for m in range(NT):
            dve.wait_ge(nm.hi, m + 1)
            nc.vector.tensor_tensor(
                self.xl[:, :, P * m:P * m + P],
                self.ps[:, s.NORM_BANK + m % 4, :].rearrange("p (c t) -> p c t", c=C),
                self.xh[:, :, P * m:P * m + P].bitcast(F32), ALU.subtract).then_inc(nm.lo, 1)
            if s.prev is not None and m + TB < NT:
                normalise(m + TB)
            if s.prev is None and m % TB == TB - 1:
                for following in range(m + 1, min(m + 1 + TB, NT)):
                    normalise(following)
            if hook is not None:
                hook(m)

    def norm_tensor(self, pe, s, hook=None):
        nc, nm = self.nc, s.norm
        for m in range(NT):
            pe.wait_ge(nm.normed, m + 1)
            after(pe, nm.lo, m - 3)
            for c in range(C):
                last = nc.tensor.transpose(self.ps[:, s.NORM_BANK + m % 4, P * c:P * c + P],
                                           self.n_xn[:, m % TB, c::C], self.ident[:])
            last.then_inc(nm.turned, 1)
            if hook is not None:
                hook(m)

    def norm_scalar(self, act, s, hook=None):
        nc, nm = self.nc, s.norm
        for m in range(NT):
            act.wait_ge(nm.turned, m + 1)
            nc.scalar.copy(self.xh[:, :, P * m:P * m + P],
                           self.ps[:, s.NORM_BANK + m % 4, :].rearrange("p (c t) -> p c t", c=C)).then_inc(nm.hi, 1)
            if hook is not None:
                hook(m)

    def half_bias(self, pool, s, b):
        nc, nm = self.nc, s.norm
        if b == 0:
            pool.wait_ge(s.bias_in, 16)
            nc.gpsimd.tensor_scalar(self.hb[:], self.hbraw[:], 0.5, None, ALU.mult).then_inc(s.halved, 1)
            pool.wait_ge(s.halved, 1)
        for m in range(TB * b, TB * b + TB):
            pool.wait_ge(nm.normed, m + 1)
            nc.gpsimd.tensor_tensor(self.x[:, m, :], self.x[:, m, :], self.hb[:],
                                    ALU.add).then_inc(nm.biased, 1)


class GatedFfn:

    STEPS = IT * BATCH
    x_new_total = STEPS * TB
    NORM_BANK = 4

    def __init__(self, pr, tag, w, w_gu_last, w_d_last, out_bias):
        self.pr, self.nc = pr, pr.nc
        self.w, self.w_gu_last, self.w_d_last = w, w_gu_last, w_d_last
        self.out_bias = out_bias
        sem = pr.sem
        self.norm = Norm(sem, f"{tag}_norm")
        self.bias_in = sem(f"{tag}_bias_in")
        self.halved = sem(f"{tag}_halved")
        self.small = sem(f"{tag}_small")
        self.zeroed = sem(f"{tag}_zeroed")
        self.tail = sem(f"{tag}_tail")
        self.raw = [sem(f"{tag}_raw{i}") for i in range(2)]
        self.w_hi = sem(f"{tag}_w_hi")
        self.w_lo = sem(f"{tag}_w_lo")
        self.gu = sem(f"{tag}_gu")
        self.silu = sem(f"{tag}_silu")
        self.h = sem(f"{tag}_h")
        self.h_hi = sem(f"{tag}_h_hi")
        self.h_lo = sem(f"{tag}_h_lo")
        self.down = sem(f"{tag}_down")
        self.x_new = sem(f"{tag}_x_new")

    def tile_ready(self, m):
        return self.x_new_total - NT + m + 1

    def gate_cols(self, c):
        return slice(P * c, P * c + P)

    def up_cols(self, c):
        return slice(P * (C + c), P * (C + c) + P)

    def sync(self, sp):
        pr = self.pr
        if self.prev is not None:
            sp.wait_ge(self.prev.x_new, self.prev.x_new_total)
        sp.dma_start(pr.hbraw[:], self.out_bias.partition_broadcast(P)).then_inc(self.bias_in, 16)
        for i in range(2):
            sp.dma_start(pr.f_raw[:, i, :], self.w[i]).then_inc(self.raw[i], 16)
        with sp.Fori(0, 4) as k:
            for par in range(2):
                sp.wait_ge(self.w_lo, k * 2 + (par + 1))
                sp.dma_start(pr.f_raw[:, par, :],
                             self.w[ds(k * 2 + (par + 2), 1)].rearrange("o p n -> p (o n)")
                             ).then_inc(self.raw[par], 16)
        gu = pr.f_raw[:, 0, 0:2 * C * P].rearrange("p (c n) -> p c n", n=P)
        down = slice(2 * C * P, FFN_W)
        sp.wait_ge(self.w_lo, IT - 2)
        sp.wait_ge(self.zeroed, 1)
        sp.dma_start(gu[:, :, I_LAST:P], pr.f_zero[:, 0:2 * C * (P - I_LAST)].rearrange(
            "p (c n) -> p c n", c=2 * C)).then_inc(self.tail, 16)
        sp.dma_start(pr.f_raw[I_LAST:P, 0, down], pr.f_zero[I_LAST:P, :]).then_inc(self.tail, 16)
        sp.dma_start(pr.f_raw[0:I_LAST, 0, down], self.w_d_last).then_inc(self.tail, 16)
        sp.wait_ge(self.tail, 48)
        sp.dma_start(gu[:, :, 0:I_LAST], self.w_gu_last).then_inc(self.raw[0], 16)

    def weights_hi(self, act, i, par, loads):
        act.wait_ge(self.raw[par], loads)
        after(act, self.down, i * 16 - 16)
        self.nc.scalar.copy(self.pr.f_bias[:, par, :], self.pr.f_raw[:, par, FFN_M:]).then_inc(self.small, 1)
        self.nc.scalar.copy(self.pr.f_hi[:, par, :], self.pr.f_raw[:, par, 0:FFN_M]).then_inc(self.w_hi, 1)

    def weights_lo(self, pool, i, par):
        pr = self.pr
        pool.wait_ge(self.w_hi, i + 1)
        self.nc.gpsimd.tensor_tensor(pr.f_lo[:, par, :], pr.f_raw[:, par, 0:FFN_M],
                                     pr.f_hi[:, par, :].bitcast(F32), ALU.subtract).then_inc(self.w_lo, 1)

    def gate_up(self, pe, t, i, s):
        pr, par, b, hp = self.pr, s // 4 % 2, s % 4, s % 2
        if b == 0:
            pe.wait_ge(self.w_lo, i + 1)
        if isinstance(t, int) and t < 4:
            pe.wait_ge(self.norm.lo, TB * (b + 1))
        after(pe, self.h, t - 1)
        tok = slice(SEQ * b, SEQ * b + SEQ)
        for bank, cols in ((2 * hp, self.gate_cols), (2 * hp + 1, self.up_cols)):
            for c in range(C):
                for a, w, x in ((0, pr.f_hi, pr.xh), (1, pr.f_hi, pr.xl), (2, pr.f_lo, pr.xh)):
                    last = self.nc.tensor.matmul(pr.ps[:, bank, :], w[:, par, cols(c)], x[:, c, tok],
                                                 start=(c == 0 and a == 0), stop=(c == C - 1 and a == 2))
        last.then_inc(self.gu, 1)

    def down_rows(self, pe, t, s):
        pr, par, hp = self.pr, s // 4 % 2, s % 2
        pe.wait_ge(self.h_lo, t + 1)
        if isinstance(t, int) and t == 0:
            pe.wait_ge(self.norm.lo, NT)
        for j in range(TB):
            after(pe, self.x_new, t * 4 + (j - 3))
            tok = slice(P * j, P * j + P)
            down = slice(2 * C * P, FFN_M)
            for a, h, w in ((0, pr.f_hh, pr.f_hi), (1, pr.f_hh, pr.f_lo), (2, pr.f_hl, pr.f_hi)):
                last = self.nc.tensor.matmul(pr.ps[:, 4 + j, :], h[:, hp, tok], w[:, par, down],
                                             start=(a == 0), stop=(a == 2))
            last.then_inc(self.down, 1)

    def tensor(self, pe):
        def hook(m):
            if m in (TB - 1, 2 * TB - 1):
                self.gate_up(pe, m // TB, 0, m // TB)

        self.pr.norm_tensor(pe, self, hook)
        for s in range(8):
            if s > 0:
                self.gate_up(pe, s + 1, (s + 1) // 4, (s + 1) % 8)
            self.down_rows(pe, s, s)
        with pe.Fori(1, IT // 2) as k:
            for s in range(8):
                self.gate_up(pe, k * 8 + (s + 1), k * 2 + (s + 1) // 4, (s + 1) % 8)
                self.down_rows(pe, k * 8 + s, s)
        for s in range(4):
            t = self.STEPS - 4 + s
            if s < 3:
                self.gate_up(pe, t + 1, IT - 1, s + 1)
            self.down_rows(pe, t, s)

    def act_step(self, act, t, i, s):
        pr, b, hp = self.pr, s % 4, s % 2
        if b == 0:
            act.wait_ge(self.small, i + 1)
        act.wait_ge(self.gu, t + 1)
        after(act, self.h, t - 1)
        self.nc.scalar.activation(pr.f_silu[:, hp, :], pr.ps[:, 2 * hp, :], ACT.Silu,
                                  bias=pr.f_bias[:, s // 4 % 2, 0:1]).then_inc(self.silu, 1)
        act.wait_ge(self.h, t + 1)
        after(act, self.down, t * 4 - 4)
        self.nc.scalar.copy(pr.f_hh[:, hp, :], pr.f_h[:, hp, :]).then_inc(self.h_hi, 1)

    def scalar(self, act):
        self.weights_hi(act, 0, 0, 16)
        self.pr.norm_scalar(act, self)
        self.weights_hi(act, 1, 1, 16)
        for s in range(8):
            self.act_step(act, s, s // 4, s)
            if s == 5:
                self.weights_hi(act, 2, 0, 32)
        with act.Fori(1, IT // 2) as k:
            for s in range(8):
                self.act_step(act, k * 8 + s, k * 2 + s // 4, s)
                if s == 1:
                    self.weights_hi(act, k * 2 + 1, 1, k * 16 + 16)
                if s == 5:
                    self.weights_hi(act, k * 2 + 2, 0, k * 16 + 32)
        for s in range(4):
            self.act_step(act, self.STEPS - 4 + s, IT - 1, s)

    def vec_h(self, dve, t, i, s):
        pr, hp = self.pr, s % 2
        dve.wait_ge(self.silu, t + 1)
        after(dve, self.h_lo, t - 1)
        self.nc.vector.scalar_tensor_tensor(out=pr.f_h[:, hp, :], in0=pr.ps[:, 2 * hp + 1, :],
                                            scalar=pr.f_bias[:, s // 4 % 2, 1:2], in1=pr.f_silu[:, hp, :],
                                            op0=ALU.add, op1=ALU.mult).then_inc(self.h, 1)

    def vec_x(self, dve, t, s):
        pr, b = self.pr, s % 4
        if isinstance(t, int) and t < BATCH:
            dve.wait_ge(self.norm.biased, TB * t + TB)
        for j in range(TB):
            dve.wait_ge(self.down, t * 4 + (j + 1))
            xm = pr.x[:, TB * b + j, :]
            self.nc.vector.scalar_tensor_tensor(out=xm, in0=pr.ps[:, 4 + j, :], scalar=0.5, in1=xm,
                                                op0=ALU.mult, op1=ALU.add).then_inc(self.x_new, 1)

    def vector(self, dve):
        self.pr.norm_vector(dve, self)
        self.vec_h(dve, 0, 0, 0)
        for s in range(8):
            self.vec_h(dve, s + 1, (s + 1) // 4, (s + 1) % 8)
            self.vec_x(dve, s, s)
        with dve.Fori(1, IT // 2) as k:
            for s in range(8):
                self.vec_h(dve, k * 8 + (s + 1), k * 2 + (s + 1) // 4, (s + 1) % 8)
                self.vec_x(dve, k * 8 + s, s)
        for s in range(4):
            t = self.STEPS - 4 + s
            if s < 3:
                self.vec_h(dve, t + 1, IT - 1, s + 1)
            self.vec_x(dve, t, s)
            dve.wait_ge(self.x_new, t * 4 + 4)
            self.pr.batch_stats(dve, self.next, s)

    def pool_step(self, pool, t, s):
        pr, hp = self.pr, s % 2
        pool.wait_ge(self.h_hi, t + 1)
        self.nc.gpsimd.tensor_tensor(pr.f_hl[:, hp, :], pr.f_h[:, hp, :], pr.f_hh[:, hp, :].bitcast(F32),
                                     ALU.subtract).then_inc(self.h_lo, 1)

    def gpsimd(self, pool):
        nc, pr = self.nc, self.pr
        if self.prev is not None:
            pool.wait_ge(self.prev.x_new, self.prev.x_new_total)
        nc.gpsimd.memset(pr.f_zero[:], 0.0).then_inc(self.zeroed, 1)
        self.weights_lo(pool, 0, 0)
        pr.half_bias(pool, self, 0)
        pr.half_bias(pool, self, 1)
        for s in range(8):
            self.pool_step(pool, s, s)
            if s == 0:
                self.weights_lo(pool, 1, 1)
            if s in (1, 2):
                pr.half_bias(pool, self, s + 1)
            if s == 5:
                self.weights_lo(pool, 2, 0)
        with pool.Fori(1, IT // 2) as k:
            for s in range(8):
                self.pool_step(pool, k * 8 + s, s)
                if s == 1:
                    self.weights_lo(pool, k * 2 + 1, 1)
                if s == 5:
                    self.weights_lo(pool, k * 2 + 2, 0)
        for s in range(4):
            self.pool_step(pool, self.STEPS - 4 + s, s)


class DequantFfn:

    x_new_total = NT
    NORM_BANK = 0
    BANKS = (4, 5, 6, 7)

    def __init__(self, pr, tag, q, zp, sc, out_bias):
        self.pr, self.nc = pr, pr.nc
        self.q, self.zp, self.sc, self.out_bias = q, zp, sc, out_bias
        sem = pr.sem
        self.norm = Norm(sem, f"{tag}_norm")
        self.bias_in = sem(f"{tag}_bias_in")
        self.halved = sem(f"{tag}_halved")
        self.coded = sem(f"{tag}_coded")
        self.codes = sem(f"{tag}_codes")
        self.wsub = sem(f"{tag}_wsub")
        self.wmul = sem(f"{tag}_wmul")
        self.w_hi = sem(f"{tag}_w_hi")
        self.w_lo = sem(f"{tag}_w_lo")
        self.y = sem(f"{tag}_y")
        self.x_new = sem(f"{tag}_x_new")

    def tile_ready(self, m):
        return m + 1

    def sync(self, sp):
        pr = self.pr
        if self.prev is not None:
            sp.wait_ge(self.prev.x_new, self.prev.x_new_total)
        sp.dma_start(pr.hbraw[:], self.out_bias.partition_broadcast(P)).then_inc(self.bias_in, 16)
        sp.dma_start(pr.d_q[:], self.q).then_inc(self.coded, 16)
        sp.dma_start(pr.d_zp[:], self.zp.partition_broadcast(P)).then_inc(self.coded, 16)
        sp.dma_start(pr.d_sc[:], self.sc.partition_broadcast(P)).then_inc(self.coded, 16)

    def vector(self, dve):
        nc, pr = self.nc, self.pr

        def weights():
            dve.wait_ge(self.coded, 48)
            for c, (word, shift) in enumerate(((0, 0), (0, 6), (1, 0), (2, 0))):
                nc.vector.tensor_scalar(pr.d_u[:, c, :], pr.d_q[:, word, :], shift, 63,
                                        ALU.arith_shift_right, ALU.bitwise_and).then_inc(self.codes, 1)
            for c in range(C):
                dve.wait_ge(self.codes, c + 1)
                nc.vector.tensor_tensor(pr.d_w[:, c, :], pr.d_u[:, c, :], pr.d_zp[:],
                                        ALU.subtract).then_inc(self.wsub, 1)
            for c in range(C):
                dve.wait_ge(self.wsub, c + 1)
                nc.vector.tensor_tensor(pr.d_w[:, c, :], pr.d_w[:, c, :], pr.d_sc[:],
                                        ALU.mult).then_inc(self.wmul, 1)
            for c in range(C):
                dve.wait_ge(self.w_hi, c + 1)
                nc.vector.tensor_tensor(pr.d_wl[:, c, :], pr.d_w[:, c, :], pr.d_wh[:, c, :].bitcast(F32),
                                        ALU.subtract).then_inc(self.w_lo, 1)

        def add(m):
            dve.wait_ge(self.norm.biased, m + 1)
            dve.wait_ge(self.y, m + 1)
            xm = pr.x[:, m, :]
            nc.vector.scalar_tensor_tensor(out=xm, in0=pr.ps[:, self.BANKS[m % 4], :], scalar=0.5,
                                           in1=xm, op0=ALU.mult, op1=ALU.add).then_inc(self.x_new, 1)
            if m % TB == TB - 1:
                dve.wait_ge(self.x_new, m + 1)
                pr.batch_stats(dve, self.next, m // TB)

        pr.norm_vector(dve, self, lambda m: add(m - TB) if m >= TB else None, meanwhile=weights)
        for m in range(NT - TB, NT):
            add(m)

    def scalar(self, act):
        nc, pr = self.nc, self.pr

        def weights(m):
            for c in range(C if m == TB - 1 else 0):
                act.wait_ge(self.wmul, c + 1)
                nc.scalar.copy(pr.d_wh[:, c, :], pr.d_w[:, c, :]).then_inc(self.w_hi, 1)

        pr.norm_scalar(act, self, weights)

    def gpsimd(self, pool):
        for b in range(BATCH):
            self.pr.half_bias(pool, self, b)

    def tensor(self, pe):
        nc, pr = self.nc, self.pr

        def product(m):
            if m == 0:
                pe.wait_ge(self.w_lo, C)
            pe.wait_ge(self.norm.lo, m + 1)
            after(pe, self.x_new, m - 3)
            tok = slice(P * m, P * m + P)
            for c in range(C):
                for a, x, w in ((0, pr.xh, pr.d_wh), (1, pr.xh, pr.d_wl), (2, pr.xl, pr.d_wh)):
                    last = nc.tensor.matmul(pr.ps[:, self.BANKS[m % 4], :], x[:, c, tok], w[:, c, :],
                                            start=(c == 0 and a == 0), stop=(c == C - 1 and a == 2))
            last.then_inc(self.y, 1)

        pr.norm_tensor(pe, self, lambda m: product(m - TB + 1) if m >= TB - 1 else None)
        for m in range(NT - TB + 1, NT):
            product(m)


class Heads:

    NORM_BANK = 0

    def __init__(self, pr, tag):
        self.pr, self.nc = pr, pr.nc
        sem = pr.sem
        self.norm = Norm(sem, f"{tag}_norm")
        self.zeroed = sem(f"{tag}_zeroed")
        self.score = sem(f"{tag}_score")
        self.max = sem(f"{tag}_max")
        self.exp = sem(f"{tag}_exp")
        self.inv = sem(f"{tag}_inv")
        self.prob = sem(f"{tag}_prob")
        self.prob2 = self.prob
        self.turn = sem(f"{tag}_turn")
        self.p_hi = sem(f"{tag}_p_hi")
        self.p_lo = sem(f"{tag}_p_lo")
        self.out = sem(f"{tag}_out")
        self.o_hi = sem(f"{tag}_o_hi")
        self.o_lo = sem(f"{tag}_o_lo")
        self.work = sem(f"{tag}_work")
        self.taken = sem(f"{tag}_taken")
        self.x_new = self.taken

    def tile_ready(self, m):
        return self.x_new_total

    def scores(self, pe, n, products, tiles=QORDER):
        pr, nc = self.pr, self.nc
        for q in tiles:
            bank, col = SBANK[q]
            if q == 0:
                after(pe, self.p_lo, n * 3)
            for a, (qt, kt) in enumerate(products):
                nc.tensor.matmul(pr.ps[:, bank, col:col + SWIDE[q]], qt[:, P * q:P * q + P],
                                 kt[:, 0:SWIDE[q]], start=(a == 0), stop=False)
            own = col + P * q
            nc.tensor.matmul(pr.ps[:, bank, own:own + P], pr.identb[:], pr.maskb[:], start=False,
                             stop=True).then_inc(self.score, 1)

    def turn_probs(self, pe, n, groups=GROUPS):
        pr, nc = self.pr, self.nc
        for tiles in groups:
            i = GROUPS.index(tiles)
            if self.prob2 is self.prob:
                pe.wait_ge(self.prob, n * 4 + (1, 2, 4)[i])
            elif tiles == (2,):
                pe.wait_ge(self.prob2, n + 1)
            else:
                pe.wait_ge(self.prob, n * 3 + (1, None, 3)[i])
            for at, q, k in ([(k, 3, k) for k in range(4)], [(k, 2, k) for k in range(3)],
                             [(0, 0, 0), (1, 1, 0), (3, 1, 1)])[i]:
                src = POFF[q] + P * k
                last = nc.tensor.transpose(pr.ps[:, TBANK["ABC"[i]], P * at:P * at + P],
                                           pr.p[:, src:src + P], pr.ident[:])
            last.then_inc(self.turn, 1)

    def attend(self, pe, n, place, v_hi, v_lo, first, end):
        pr, nc = self.pr, self.nc
        th, tl = self.turned_parts(place)
        pe.wait_ge(self.p_lo, n * 3 + 3)
        for k in range(TB):
            lo = min(k, TB - 2) * P
            for a, v, p in ((0, v_hi, th), (1, v_lo, th), (2, v_hi, tl)):
                last = nc.tensor.matmul(pr.ps[:, OBANK, lo:SEQ], v(k), p[:, k, lo:SEQ],
                                        start=(first and k == 0 and a == 0),
                                        stop=(end and k == TB - 1 and a == 2))
        return last

    def maxima(self, dve, n, tiles=QORDER):
        pr, nc = self.pr, self.nc
        for q in tiles:
            if q != 1:
                dve.wait_ge(self.score, n * 4 + {3: 1, 2: 2, 0: 4}[q])
            bank, col = SBANK[q]
            nc.vector.tensor_reduce(pr.nmax[:, q:q + 1], pr.ps[:, bank, col:col + P * (q + 1)], AX.X,
                                    ALU.max, negate=True).then_inc(self.max, 1)

    def normalise(self, dve, n, pairs=(0, 1)):
        pr, nc = self.pr, self.nc
        for i in pairs:
            tiles = QORDER[2 * i:2 * i + 2]
            both = slice(min(tiles), max(tiles) + 1)
            dve.wait_ge(self.exp, n * 4 + (2 * i + 2))
            nc.vector.reciprocal(pr.rsum[:, both], pr.psum_[:, both]).then_inc(self.inv, 1)
            dve.wait_ge(self.inv, n * 2 + (i + 1))
            for q in tiles:
                if q == 2 and self.prob2 is not self.prob:
                    continue
                p = pr.p[:, POFF[q]:POFF[q] + P * (q + 1)]
                nc.vector.tensor_scalar(p, p, pr.rsum[:, q:q + 1], None, ALU.mult).then_inc(self.prob, 1)

    def turned_parts(self, place):
        return self.pr.pth, self.pr.ptl

    def turned_views(self, i, dst):
        ps = self.pr.ps
        if i == 0:
            return ps[:, TBANK["A"], :].rearrange("p (k t) -> p k t", k=4), dst[:, :, 3 * P:4 * P]
        if i == 1:
            return (ps[:, TBANK["B"], 0:3 * P].rearrange("p (k t) -> p k t", k=3), dst[:, 0:3, 2 * P:3 * P])
        return ps[:, TBANK["C"], :].rearrange("p (k t) -> p k t", k=2), dst[:, 0:2, 0:2 * P]

    def probs_lo(self, dve, n, place):
        th, tl = self.turned_parts(place)
        for i in range(3):
            dve.wait_ge(self.p_hi, n * 3 + (i + 1))
            src, lo = self.turned_views(i, tl)
            _, hi = self.turned_views(i, th)
            self.nc.vector.tensor_tensor(lo, src, hi.bitcast(F32), ALU.subtract).then_inc(self.p_lo, 1)

    def exponentials(self, act, n, tiles=QORDER):
        pr, nc = self.pr, self.nc
        for q in tiles:
            if q != 1:
                act.wait_ge(self.max, n * 4 + {3: 1, 2: 2, 0: 4}[q])
            bank, col = SBANK[q]
            w = P * (q + 1)
            nc.scalar.activation(pr.p[:, POFF[q]:POFF[q] + w], pr.ps[:, bank, col:col + w], ACT.Exp,
                                 bias=pr.nmax[:, q:q + 1],
                                 accum_out=pr.psum_[:, q:q + 1]).then_inc(self.exp, 1)

    def probs_hi(self, act, n, place, parts=range(3)):
        for i in parts:
            act.wait_ge(self.turn, n * 3 + (i + 1))
            src, hi = self.turned_views(i, self.turned_parts(place)[0])
            self.nc.scalar.copy(hi, src).then_inc(self.p_hi, 1)

    def clear(self, pool, more):
        pr, nc = self.pr, self.nc
        regions = more + [pr.pth[:, 3, 2 * P:3 * P].bitcast(F32),
                          pr.ptl[:, 3, 2 * P:3 * P].bitcast(F32)]
        if self.prev is not None:
            pool.wait_ge(self.prev.x_new, self.prev.x_new_total)
        for i, r in enumerate(regions):
            if i == len(more):
                pool.wait_ge(self.norm.lo, NT)
            after(pool, self.zeroed, i)
            nc.gpsimd.memset(r, 0.0).then_inc(self.zeroed, 1)
        self.cleared = len(regions)

    def x_tile(self, m):
        return self.pr.x[:].rearrange("p t d -> p (t d)")[:, ds(m * D, D)]


class SmallHeads(Heads):

    x_new_total = UNITS0 * 7
    Q_SCALE = HD0 ** -0.5
    COPIES = (UH + 2 * UKV) * 3

    def __init__(self, pr, tag):
        super().__init__(pr, tag)
        sem = pr.sem
        self.prob2 = sem(f"{tag}_prob2")
        self.qkv_in = sem(f"{tag}_qkv_in")
        self.qkv_hi = sem(f"{tag}_qkv_hi")
        self.qkv_lo = sem(f"{tag}_qkv_lo")
        self.wo_in = sem(f"{tag}_wo_in")
        self.wo_hi = sem(f"{tag}_wo_hi")
        self.wo_lo = sem(f"{tag}_wo_lo")
        self.q_hi = sem(f"{tag}_q_hi")
        self.k_hi = sem(f"{tag}_k_hi")
        self.v_hi = sem(f"{tag}_v_hi")
        self.spread = sem(f"{tag}_spread")

    AHEAD = {"q": 0, "kv": 1}
    ORDER_FIRST = {"vt": 0, "q": 1, "kv": 2}
    ORDER = {"vt": 0, "q": 1, "kv": 2, "y0": 3, "y1": 4, "y2": 5, "y3": 6}
    ORDER_LAST = {"vt": 0, "y0": 1, "y1": 2, "y2": 3, "y3": 4, "end0": 5, "end1": 6, "end2": 7, "end3": 8}

    def item(self, u, kind):
        if isinstance(u, int) and u == 0:
            return len(self.AHEAD) + self.ORDER_FIRST[kind]
        order = self.ORDER_LAST if isinstance(u, int) and u == UNITS0 - 1 else self.ORDER
        return u * 7 + (order[kind] - 2)

    def bank(self, u, par, kind):
        if isinstance(u, int):
            return WBANK[self.item(u, kind) % 2]
        return WBANK[(par * 7 + self.ORDER[kind]) % 2]

    def turned_parts(self, place):
        pr = self.pr
        return ((pr.pth, pr.ptl), (pr.a_pth, pr.a_ptl))[place % 2]

    def x_of(self, u, part, c):
        col = (u & 3) * SEQ
        return part[:, c, ds(col, SEQ)]

    RESULTS = {5: ("y0",), 6: ("y1",), 7: ("y2", "y3")}

    def project(self, pe, u, w, bank, cols, chunks=range(C)):
        pr = self.pr
        if chunks[0] == 0:
            pe.wait_ge(self.norm.lo, TB if isinstance(u, int) and u == 0 else NT)
            after(pe, self.taken, w - 1)
            pe.wait_ge(self.qkv_lo, u + 1)
        step = QCOL + P
        for c in chunks:
            at = slice(step * c + cols, step * c + cols + P)
            for a, wt, x in ((0, pr.a_wh, pr.xh), (1, pr.a_wh, pr.xl), (2, pr.a_wl, pr.xh)):
                last = self.nc.tensor.matmul(pr.ps[:, bank, :], wt[:, at], self.x_of(u, x, c),
                                             start=(c == 0 and a == 0), stop=(c == C - 1 and a == 2))
        if chunks[-1] == C - 1:
            last.then_inc(self.work, 1)

    def turn_values(self, pe, u, w, bank, w_kv):
        pr = self.pr
        pe.wait_ge(pr.consts, 5)
        pe.wait_ge(self.taken, w_kv + 1)
        after(pe, self.taken, w - 1)
        for k in range(TB):
            last = self.nc.tensor.transpose(pr.ps[:, bank, P * k:P * k + P], pr.a_kh[:, P * k:P * k + P].bitcast(F32),
                                            pr.ident[:])
        last.then_inc(self.work, 1)

    def result(self, pe, u, w, bank, j):
        pr = self.pr
        if j == 0:
            pe.wait_ge(self.o_lo, u + 1)
            pe.wait_ge(self.wo_lo, u + 1)
        after(pe, self.taken, w - 1)
        tok = slice(P * j, P * j + P)
        for a, o, wt in ((0, pr.a_oth, pr.a_oh), (1, pr.a_oth, pr.a_ol), (2, pr.a_otl, pr.a_oh)):
            last = self.nc.tensor.matmul(pr.ps[:, bank, :], o[:, tok], wt[:], start=(a == 0), stop=(a == 2))
        last.then_inc(self.work, 1)

    def values(self, pe, n, u, j, vt_item):
        pr = self.pr
        if j == 0:
            pe.wait_ge(self.taken, vt_item + 1)
            after(pe, self.o_lo, u)
        at = VWIN - P - HD0 * j
        kv = j // (UH // UKV)
        last = self.attend(pe, n, j, lambda k: pr.a_vh[:, kv, k, at:at + P], lambda k: pr.a_vl[:, kv, k, at:at + P],
                           first=(j == 0), end=(j == UH - 1))
        if j == UH - 1:
            last.then_inc(self.out, 1)

    def products(self, par, j):
        pr = self.pr
        if j >= UH:
            par, j = 1 - par, j - UH
        return [(pr.a_q2[:, par, j // 2, :], pr.a_k2[:, par, j % 2, j // (UH // UKV), :])]

    def unit_tensor(self, pe, u, par, first=False, last=False):
        for j in range(UH):
            n = u * UH + j
            more = not (last and j == UH - 1)
            if j <= 3 and not last:
                kind, cols = ("q", QCOL) if j <= 1 else ("kv", 0)
                half = range(C // 2, C) if j % 2 else range(0, C // 2)
                self.project(pe, u + 1, self.item(u, kind), self.bank(u, par, kind), cols, half)
            if not first:
                for kind in self.RESULTS.get(j, ()):
                    self.result(pe, u - 1, self.item(u, kind), self.bank(u, par, kind), int(kind[1]))
            self.turn_probs(pe, n, GROUPS[2:])
            if j > 0:
                self.values(pe, n - 1, u, j - 1, self.item(u, "vt"))
            elif not first:
                self.values(pe, n - 1, u - 1, UH - 1, None)
            if j == 0:
                self.turn_values(pe, u, self.item(u, "vt"), self.bank(u, par, "vt"),
                                 self.AHEAD["kv"] if first else self.item(u - 1, "kv"))
            if more:
                self.scores(pe, n + 1, self.products(par, j + 1), QORDER[2:])
            if not (last and j >= UH - 2):
                if j == UH - 2:
                    pe.wait_ge(self.spread, u * (16 * self.COPIES) + 2 * 16 * self.COPIES)
                pe.wait_ge(self.exp, n * 4 + 6)
                self.scores(pe, n + 2, self.products(par, j + 2), QORDER[:2])
            if more:
                self.turn_probs(pe, n + 1, GROUPS[:2])

    def tensor(self, pe):
        def hook(m):
            if m == TB - 1:
                self.project(pe, 0, self.AHEAD["q"], WBANK[0], QCOL)
                self.project(pe, 0, self.AHEAD["kv"], WBANK[1], 0)

        self.pr.norm_tensor(pe, self, hook)
        pe.wait_ge(self.norm.lo, NT)
        pe.wait_ge(self.zeroed, self.n_zero)
        pe.wait_ge(self.spread, 16 * self.COPIES)
        self.scores(pe, 0, self.products(0, 0))
        pe.wait_ge(self.exp, 2)
        self.scores(pe, 1, self.products(0, 1), QORDER[:2])
        self.turn_probs(pe, 0, GROUPS[:2])
        self.unit_tensor(pe, 0, 0, first=True)
        self.unit_tensor(pe, 1, 1)
        with pe.Fori(1, UNITS0 // 2 - 1) as k:
            self.unit_tensor(pe, k * 2, 0)
            self.unit_tensor(pe, k * 2 + 1, 1)
        self.unit_tensor(pe, UNITS0 - 2, 0)
        u = UNITS0 - 1
        self.unit_tensor(pe, u, 1, last=True)
        self.values(pe, u * UH + UH - 1, u, UH - 1, None)
        for t in range(TB):
            self.result(pe, u, self.item(u, f"end{t}"), self.bank(u, 1, f"end{t}"), t)

    n_zero = 8

    def take_q(self, dve, u, bank):
        pr = self.pr
        dve.wait_ge(self.q_hi, u + 1)
        self.nc.vector.scalar_tensor_tensor(out=pr.a_ql[:], in0=pr.ps[:, bank, :], scalar=self.Q_SCALE,
                                            in1=pr.a_qh[:].bitcast(F32), op0=ALU.mult,
                                            op1=ALU.subtract).then_inc(self.taken, 1)

    def take_kv(self, dve, u, bank):
        pr, n = self.pr, UKV * HD0
        dve.wait_ge(self.k_hi, u + 1)
        self.nc.vector.tensor_tensor(pr.a_kl[n:2 * n, :], pr.ps[n:2 * n, bank, :],
                                     pr.a_kh[n:2 * n, :].bitcast(F32), ALU.subtract)
        self.nc.vector.tensor_copy(pr.a_kh[0:n, :].bitcast(F32), pr.ps[0:n, bank, :]).then_inc(self.taken, 1)

    def value_views(self, bank, kv, dst):
        src = self.pr.ps[:, bank, :].rearrange("p (k n) -> p k n", k=TB)
        return src[:, :, HD0 * kv:HD0 * kv + HD0], dst[:, kv, :, VWIN - P:VWIN - P + HD0]

    def take_vt(self, dve, u, bank):
        pr = self.pr
        dve.wait_ge(self.v_hi, u * UKV + UKV)
        for kv in range(UKV):
            src, lo = self.value_views(bank, kv, pr.a_vl)
            _, hi = self.value_views(bank, kv, pr.a_vh)
            ins = self.nc.vector.tensor_tensor(lo, src, hi.bitcast(F32), ALU.subtract)
        ins.then_inc(self.taken, 1)

    def take_out(self, dve, u):
        pr = self.pr
        dve.wait_ge(self.o_hi, u + 1)
        self.nc.vector.tensor_tensor(pr.a_otl[:], pr.ps[:, OBANK, :], pr.a_oth[:].bitcast(F32),
                                     ALU.subtract).then_inc(self.o_lo, 1)

    def take_result(self, dve, u, w, bank, t):
        dve.wait_ge(self.work, w + 1)
        xm = self.x_tile((u & 3) * TB + t)
        self.nc.vector.tensor_tensor(xm, self.pr.ps[:, bank, :], xm,
                                     ALU.add).then_inc(self.taken, 1)

    def unit_vector(self, dve, u, par, first=False, last=False):
        for j in range(UH):
            n = u * UH + j
            more = not (last and j == UH - 1)
            self.probs_lo(dve, n, j)
            if j == 1 and not last:
                self.take_q(dve, u + 1, self.bank(u, par, "q"))
            if j == 3 and not last:
                self.take_kv(dve, u + 1, self.bank(u, par, "kv"))
            if more:
                self.normalise(dve, n + 1, (0,))
            if not first:
                for kind in self.RESULTS.get(j, ()):
                    self.take_result(dve, u - 1, self.item(u, kind), self.bank(u, par, kind), int(kind[1]))
            if j == 0:
                if not first:
                    self.take_out(dve, u - 1)
                self.take_vt(dve, u, self.bank(u, par, "vt"))
            if more:
                self.maxima(dve, n + 1, QORDER[2:])
                if not (last and j == UH - 2):
                    self.maxima(dve, n + 2, QORDER[:2])
                self.normalise(dve, n + 1, (1,))
            if j == UH - 1 and isinstance(u, int) and u >= UNITS0 - 2:
                dve.wait_ge(self.taken, self.item(u, "y3") + 1)
                for b in range(2 * (u - (UNITS0 - 2)), u - (UNITS0 - 2) + 2):
                    self.pr.batch_stats(dve, self.next, b)

    def vector(self, dve):
        def hook(m):
            if m == TB - 1:
                self.take_q(dve, 0, WBANK[0])
                self.take_kv(dve, 0, WBANK[1])

        self.pr.norm_vector(dve, self, hook)
        self.maxima(dve, 0)
        self.normalise(dve, 0, (0,))
        self.maxima(dve, 1, QORDER[:2])
        self.normalise(dve, 0, (1,))
        self.unit_vector(dve, 0, 0, first=True)
        self.unit_vector(dve, 1, 1)
        with dve.Fori(1, UNITS0 // 2 - 1) as k:
            self.unit_vector(dve, k * 2, 0)
            self.unit_vector(dve, k * 2 + 1, 1)
        self.unit_vector(dve, UNITS0 - 2, 0)
        u = UNITS0 - 1
        self.unit_vector(dve, u, 1, last=True)
        self.take_out(dve, u)
        for t in range(TB):
            self.take_result(dve, u, self.item(u, f"end{t}"), self.bank(u, 1, f"end{t}"), t)
        dve.wait_ge(self.taken, self.x_new_total)
        self.pr.batch_stats(dve, self.next, BATCH - 1)

    def split_qkv(self, act, u):
        act.wait_ge(self.qkv_in, u * 16 + 16)
        self.nc.scalar.copy(self.pr.a_wh[:], self.pr.a_raw[:]).then_inc(self.qkv_hi, 1)

    def split_wo(self, act, u, last_use):
        if last_use is not None:
            act.wait_ge(self.work, last_use + 1)
        act.wait_ge(self.wo_in, u * 16 + 16)
        self.nc.scalar.copy(self.pr.a_oh[:], self.pr.a_raw[:, 0:D]).then_inc(self.wo_hi, 1)

    def hi_q(self, act, u, w, bank):
        act.wait_ge(self.work, w + 1)
        after(act, self.spread, u * (16 * self.COPIES))
        self.nc.scalar.activation(self.pr.a_qh[:], self.pr.ps[:, bank, :], ACT.Copy,
                                  scale=self.Q_SCALE).then_inc(self.q_hi, 1)

    def hi_kv(self, act, u, w, bank):
        act.wait_ge(self.work, w + 1)
        self.nc.scalar.copy(self.pr.a_kh[:], self.pr.ps[:, bank, :]).then_inc(self.k_hi, 1)

    def hi_vt(self, act, w, bank):
        act.wait_ge(self.work, w + 1)
        for kv in range(UKV):
            src, hi = self.value_views(bank, kv, self.pr.a_vh)
            self.nc.scalar.copy(hi, src).then_inc(self.v_hi, 1)

    def hi_out(self, act, u):
        act.wait_ge(self.out, u + 1)
        self.nc.scalar.copy(self.pr.a_oth[:], self.pr.ps[:, OBANK, :]).then_inc(self.o_hi, 1)

    def normalise_tile2(self, act, n):
        pr = self.pr
        act.wait_ge(self.inv, n * 2 + 1)
        p = pr.p[:, POFF[2]:POFF[2] + P * 3]
        self.nc.scalar.activation(p, p, ACT.Copy, scale=pr.rsum[:, 2:3]).then_inc(self.prob2, 1)

    def unit_scalar(self, act, u, par, first=False, last=False, last2=False):
        for j in range(UH):
            n = u * UH + j
            more = not (last and j == UH - 1)
            self.probs_hi(act, n, j, (0, 1))
            if more:
                self.exponentials(act, n + 1, QORDER[:1])
            self.probs_hi(act, n, j, (2,))
            if j == 1 and not last:
                self.hi_q(act, u + 1, self.item(u, "q"), self.bank(u, par, "q"))
            if j == 3 and not last:
                self.hi_kv(act, u + 1, self.item(u, "kv"), self.bank(u, par, "kv"))
            if more:
                self.exponentials(act, n + 1, QORDER[1:2])
                self.normalise_tile2(act, n + 1)
            if j == 0:
                if not first:
                    self.hi_out(act, u - 1)
                self.hi_vt(act, self.item(u, "vt"), self.bank(u, par, "vt"))
            if more:
                self.exponentials(act, n + 1, QORDER[2:])
            if j == 2 and not first:
                second = isinstance(u, int) and u == 1
                self.split_wo(act, u - 1, None if second else self.item(u - 1, "y3"))
            if j == 4 and not (last or last2):
                self.split_qkv(act, u + 2)

    def scalar(self, act):
        self.split_qkv(act, 0)

        def hook(m):
            if m == TB - 1:
                self.hi_q(act, 0, self.AHEAD["q"], WBANK[0])
                self.hi_kv(act, 0, self.AHEAD["kv"], WBANK[1])

        self.pr.norm_scalar(act, self, hook)
        self.split_qkv(act, 1)
        self.exponentials(act, 0)
        self.normalise_tile2(act, 0)
        self.unit_scalar(act, 0, 0, first=True)
        self.unit_scalar(act, 1, 1)
        with act.Fori(1, UNITS0 // 2 - 1) as k:
            self.unit_scalar(act, k * 2, 0)
            self.unit_scalar(act, k * 2 + 1, 1)
        self.unit_scalar(act, UNITS0 - 2, 0, last2=True)
        self.unit_scalar(act, UNITS0 - 1, 1, last=True)
        self.split_wo(act, UNITS0 - 1, self.item(UNITS0 - 1, "y3"))
        self.hi_out(act, UNITS0 - 1)

    def lo_qkv(self, pool, u):
        pr = self.pr
        pool.wait_ge(self.qkv_hi, u + 1)
        self.nc.gpsimd.tensor_tensor(pr.a_wl[:], pr.a_raw[:], pr.a_wh[:].bitcast(F32),
                                     ALU.subtract).then_inc(self.qkv_lo, 1)

    def lo_wo(self, pool, u):
        pr = self.pr
        pool.wait_ge(self.wo_hi, u + 1)
        self.nc.gpsimd.tensor_tensor(pr.a_ol[:], pr.a_raw[:, 0:D], pr.a_oh[:].bitcast(F32),
                                     ALU.subtract).then_inc(self.wo_lo, 1)

    def gpsimd(self, pool):
        pr = self.pr
        self.lo_qkv(pool, 0)
        self.clear(pool, [x.bitcast(F32) for x in (
            pr.a_k2[:], pr.a_q2[:], pr.a_vh[:], pr.a_vl[:],
            pr.a_pth[:, 3, 2 * P:3 * P], pr.a_ptl[:, 3, 2 * P:3 * P])])
        assert self.cleared == self.n_zero
        self.lo_qkv(pool, 1)
        self.lo_qkv(pool, 2)
        self.lo_wo(pool, 0)
        self.lo_qkv(pool, 3)
        with pool.Fori(1, UNITS0 // 2 - 1) as k:
            for s in range(2):
                self.lo_wo(pool, k * 2 + (s - 1))
                self.lo_qkv(pool, k * 2 + (s + 2))
        for u in range(UNITS0 - 3, UNITS0):
            self.lo_wo(pool, u)

    def spread_q(self, sp, w, par):
        pr = self.pr
        sp.wait_ge(self.taken, w + 1)
        for h in range(UH):
            for r in range(3):
                at = P // 2 * (h % 2) + HD0 * r
                part = (pr.a_qh, pr.a_ql)[r % 2]
                sp.dma_start(pr.a_q2[at:at + HD0, par, h // 2, :].bitcast(F32),
                             part[HD0 * h:HD0 * h + HD0, :].bitcast(F32)).then_inc(self.spread, 16)

    def spread_k(self, sp, w, par):
        pr = self.pr
        sp.wait_ge(self.taken, w + 1)
        for kv in range(UKV):
            for half in range(2):
                for r in range(3):
                    at = P // 2 * half + HD0 * r
                    src = UKV * HD0 + HD0 * kv
                    part = (pr.a_kh, pr.a_kl)[r // 2]
                    sp.dma_start(pr.a_k2[at:at + HD0, par, half, kv, :].bitcast(F32),
                                 part[src:src + HD0, :].bitcast(F32)).then_inc(self.spread, 16)

    def chunk_sync(self, sp, c, last=False):
        pr = self.pr
        for b in range(BATCH):
            u = c * BATCH + b
            if not (last and b + 1 >= BATCH):
                self.spread_q(sp, self.item(u, "q"), 1 - b % 2)
            if not (last and b + 2 >= BATCH):
                if isinstance(u, int) and u == 0:
                    sp.wait_ge(self.qkv_lo, 2)
                else:
                    sp.wait_ge(self.wo_lo, u)
                rows = c * P + (P if b + 2 >= BATCH else 0)
                sp.dma_start(pr.a_raw[:], pr.io["at0_qkv"][ds(rows, P), :]).then_inc(self.qkv_in, 16)
            if not (last and b + 1 >= BATCH):
                self.spread_k(sp, self.item(u, "kv"), 1 - b % 2)
            if last and b + 2 >= BATCH:
                sp.wait_ge(self.wo_lo, u)
            else:
                sp.wait_ge(self.qkv_lo, u + 3)
            sp.dma_start(pr.a_raw[:, 0:D], pr.io["at0_o"][ds(c * P, P), :]).then_inc(self.wo_in, 16)

    def sync(self, sp):
        pr = self.pr
        if self.prev is not None:
            sp.wait_ge(self.prev.x_new, self.prev.x_new_total)
        sp.dma_start(pr.a_raw[:], pr.io["at0_qkv"][0:P, :]).then_inc(self.qkv_in, 16)
        sp.wait_ge(self.qkv_lo, 1)
        sp.dma_start(pr.a_raw[:], pr.io["at0_qkv"][0:P, :]).then_inc(self.qkv_in, 16)
        sp.wait_ge(self.zeroed, 2)
        self.spread_q(sp, self.AHEAD["q"], 0)
        self.spread_k(sp, self.AHEAD["kv"], 0)
        self.chunk_sync(sp, 0)
        with sp.Fori(1, C - 1) as c:
            self.chunk_sync(sp, c)
        self.chunk_sync(sp, C - 1, last=True)


class RopeHeads(Heads):

    x_new_total = UNITS1 * 11

    def __init__(self, pr, tag):
        super().__init__(pr, tag)
        sem = pr.sem
        self.tables_in = sem(f"{tag}_tables_in")
        self.w_in = sem(f"{tag}_w_in")
        self.w_hi = sem(f"{tag}_w_hi")
        self.w_lo = sem(f"{tag}_w_lo")
        self.swap = sem(f"{tag}_swap")
        self.sine = sem(f"{tag}_sine")
        self.turned = sem(f"{tag}_turned")
        self.t_hi = sem(f"{tag}_t_hi")
        self.t_lo = sem(f"{tag}_t_lo")
        self.v_hi = sem(f"{tag}_v_hi")

    AHEAD = {"k": 0, "v": 1, "q0": 2, "q1": 3, "vt": 4}
    ORDER_FIRST = {"q0": 0, "q1": 1, "k": 2, "q2": 3, "v": 4, "q3": 5, "vt": 6}
    ORDER = {"q0": 0, "y": 1, "q1": 5, "k": 6, "q2": 7, "v": 8, "q3": 9, "vt": 10, "end": 6}

    def item(self, u, kind, j=0):
        if isinstance(u, int) and u == 0:
            return len(self.AHEAD) + self.ORDER_FIRST[kind]
        return u * 11 + (self.ORDER[kind] + j + 1)

    def bank(self, u, par, kind, j=0):
        if isinstance(u, int):
            return WBANK[self.item(u, kind, j) % 2]
        return WBANK[(par * 11 + self.ORDER[kind] + j + 1) % 2]

    @staticmethod
    def rotation(u, kind):
        return u * 5 + (3 + {"q0": 0, "q1": 1, "k": 2, "q2": 3, "q3": 4}[kind])

    def project(self, pe, w, bank, piece, need, batch):
        pr = self.pr
        pe.wait_ge(self.w_lo, need)
        after(pe, self.taken, w - 1)
        tok = slice(SEQ * batch, SEQ * batch + SEQ)
        for c in range(C):
            for a, wt, x in ((0, pr.r_wh, pr.xh), (1, pr.r_wh, pr.xl), (2, pr.r_wl, pr.xh)):
                last = self.nc.tensor.matmul(pr.ps[:, bank, :], wt[:, piece, P * c:P * c + P], x[:, c, tok],
                                             start=(c == 0 and a == 0), stop=(c == C - 1 and a == 2))
        last.then_inc(self.work, 1)

    def turn_values(self, pe, w, bank, w_v):
        pr = self.pr
        pe.wait_ge(self.taken, w_v + 1)
        after(pe, self.taken, w - 1)
        for k in range(TB):
            last = self.nc.tensor.transpose(pr.ps[:, bank, P * k:P * k + P], pr.r_vt[:, P * k:P * k + P],
                                            pr.ident[:])
        last.then_inc(self.work, 1)

    def results(self, pe, u, need, items):
        pr = self.pr
        pe.wait_ge(self.o_lo, u * R1 + R1)
        pe.wait_ge(self.w_lo, need)
        for t, (w, bank) in enumerate(items):
            after(pe, self.taken, w - 1)
            tok = slice(P * t, P * t + P)
            for h in range(R1):
                o = PIECES - R1 + h
                for a, x, wt in ((0, pr.r_oth, pr.r_wh), (1, pr.r_oth, pr.r_wl), (2, pr.r_otl, pr.r_wh)):
                    last = self.nc.tensor.matmul(pr.ps[:, bank, :], x[:, h, tok], wt[:, o, :],
                                                 start=(h == 0 and a == 0), stop=(h == R1 - 1 and a == 2))
            last.then_inc(self.work, 1)

    def output(self, pe, n):
        pr = self.pr
        after(pe, self.o_lo, n)
        self.attend(pe, n, None, lambda k: pr.r_vh[:, k, :], lambda k: pr.r_vl[:, k, :],
                    first=True, end=True).then_inc(self.out, 1)

    def head_scores(self, pe, u, par, j):
        pr = self.pr
        pe.wait_ge(self.t_lo, u * 5 + (2 + j))
        self.scores(pe, u * R1 + j, [(pr.r_qh[:, j % 2, :], pr.r_kh[:, par, :]),
                                     (pr.r_qh[:, j % 2, :], pr.r_kl[:, par, :]),
                                     (pr.r_ql[:, j % 2, :], pr.r_kh[:, par, :])])

    def group_tensor(self, pe, g, first=False, last=False):
        for b in range(BATCH):
            u, par = g * BATCH + b, b % 2
            u_first, u_last = first and b == 0, last and b == BATCH - 1
            nb, ng = (b + 1) % BATCH, g + (b + 1) // BATCH
            for j in range(R1):
                n = u * R1 + j
                self.turn_probs(pe, n)
                if not (u_last and j >= 2):
                    q = (j + 2) % R1
                    self.project(pe, self.item(u, f"q{j}"), self.bank(u, par, f"q{j}"), 2 + q,
                                 (g if j < 2 else ng) * PIECES + (3 + q), b if j < 2 else nb)
                if j < R1 - 1:
                    self.head_scores(pe, u, par, j + 1)
                elif not u_last:
                    self.head_scores(pe, u + 1, 1 - par, 0)
                if j == 0:
                    vt = self.AHEAD["vt"] if u_first else self.item(u - 1, "vt")
                    pe.wait_ge(self.taken, vt + 1)
                self.output(pe, n)
                if j == 0 and not u_first:
                    self.results(pe, u - 1, (g if b == 0 else g + 1) * PIECES,
                                 [(self.item(u, "y", t), self.bank(u, par, "y", t)) for t in range(TB)])
                if j == 1 and not u_last:
                    self.project(pe, self.item(u, "k"), self.bank(u, par, "k"), 0, ng * PIECES + 1, nb)
                if j == 2 and not u_last:
                    self.project(pe, self.item(u, "v"), self.bank(u, par, "v"), 1, ng * PIECES + 2, nb)
                if j == 3 and not u_last:
                    self.turn_values(pe, self.item(u, "vt"), self.bank(u, par, "vt"), self.item(u, "v"))

    def tensor(self, pe):
        def ahead(kind, piece):
            w = self.AHEAD[kind]
            self.project(pe, w, WBANK[w % 2], piece, piece + 1, 0)

        def hook(m):
            if m == TB - 1:
                pe.wait_ge(self.norm.lo, TB)
                ahead("k", 0)
                ahead("v", 1)

        self.pr.norm_tensor(pe, self, hook)
        pe.wait_ge(self.norm.lo, NT)
        ahead("q0", 2)
        ahead("q1", 3)
        w = self.AHEAD["vt"]
        self.turn_values(pe, w, WBANK[w % 2], self.AHEAD["v"])
        pe.wait_ge(self.zeroed, self.n_zero)
        self.head_scores(pe, 0, 0, 0)
        self.group_tensor(pe, 0, first=True)
        with pe.Fori(1, G1 - 1) as g:
            self.group_tensor(pe, g)
        self.group_tensor(pe, G1 - 1, last=True)
        u = UNITS1 - 1
        self.results(pe, u, G1 * PIECES, [(self.item(u, "end", t), self.bank(u, 1, "end", t)) for t in range(TB)])

    n_zero = 2

    def rotate(self, dve, r, bank):
        pr, nc = self.pr, self.nc
        dve.wait_ge(self.swap, r + 1)
        after(dve, self.t_lo, r)
        nc.vector.tensor_tensor(pr.r_t[:], pr.ps[:, bank, :], pr.r_cos[:], ALU.mult).then_inc(self.taken, 1)
        nc.vector.tensor_tensor(pr.r_sw[:], pr.r_sw[:], pr.r_sin[:], ALU.mult).then_inc(self.sine, 1)

    def take_v(self, dve, w, bank):
        dve.wait_ge(self.work, w + 1)
        self.nc.vector.tensor_copy(self.pr.r_vt[:], self.pr.ps[:, bank, :]).then_inc(self.taken, 1)

    def take_vt(self, dve, u, bank):
        pr = self.pr
        dve.wait_ge(self.v_hi, u + 1)
        self.nc.vector.tensor_tensor(pr.r_vl[:], pr.ps[:, bank, :].rearrange("p (k d) -> p k d", k=TB),
                                     pr.r_vh[:].bitcast(F32), ALU.subtract).then_inc(self.taken, 1)

    def take_out(self, dve, n, j):
        pr = self.pr
        dve.wait_ge(self.o_hi, n + 1)
        self.nc.vector.tensor_tensor(pr.r_otl[:, j, :], pr.ps[:, OBANK, :], pr.r_oth[:, j, :].bitcast(F32),
                                     ALU.subtract).then_inc(self.o_lo, 1)

    def take_result(self, dve, m, w, bank):
        dve.wait_ge(self.work, w + 1)
        xm = self.pr.x[:, m, :]
        self.nc.vector.tensor_tensor(xm, self.pr.ps[:, bank, :], xm, ALU.add).then_inc(self.taken, 1)

    def group_vector(self, dve, g, first=False, last=False):
        for b in range(BATCH):
            u, par = g * BATCH + b, b % 2
            u_first, u_last = first and b == 0, last and b == BATCH - 1
            for j in range(R1):
                n = u * R1 + j
                self.probs_lo(dve, n, j)
                if not (u_last and j >= 2):
                    self.rotate(dve, self.rotation(u, f"q{j}"), self.bank(u, par, f"q{j}"))
                if not (u_last and j == R1 - 1):
                    self.maxima(dve, n + 1)
                    self.normalise(dve, n + 1)
                if j == 0 and not u_first:
                    for t in range(TB):
                        self.take_result(dve, TB * ((b - 1) % BATCH) + t, self.item(u, "y", t),
                                         self.bank(u, par, "y", t))
                    if last and b > 0:
                        dve.wait_ge(self.taken, self.item(u, "y", TB - 1) + 1)
                        self.pr.batch_stats(dve, self.next, b - 1)
                self.take_out(dve, n, j)
                if j == 1 and not u_last:
                    self.rotate(dve, self.rotation(u, "k"), self.bank(u, par, "k"))
                if j == 2 and not u_last:
                    self.take_v(dve, self.item(u, "v"), self.bank(u, par, "v"))
                if j == 3 and not u_last:
                    self.take_vt(dve, u + 1, self.bank(u, par, "vt"))

    def vector(self, dve):
        self.pr.norm_vector(dve, self)
        dve.wait_ge(self.tables_in, 2 * 16)
        self.rotate(dve, 0, WBANK[self.AHEAD["k"] % 2])
        self.take_v(dve, self.AHEAD["v"], WBANK[self.AHEAD["v"] % 2])
        self.rotate(dve, 1, WBANK[self.AHEAD["q0"] % 2])
        self.rotate(dve, 2, WBANK[self.AHEAD["q1"] % 2])
        self.take_vt(dve, 0, WBANK[self.AHEAD["vt"] % 2])
        self.maxima(dve, 0)
        self.normalise(dve, 0)
        self.group_vector(dve, 0, first=True)
        with dve.Fori(1, G1 - 1) as g:
            self.group_vector(dve, g)
        self.group_vector(dve, G1 - 1, last=True)
        u = UNITS1 - 1
        for t in range(TB):
            self.take_result(dve, TB * (BATCH - 1) + t, self.item(u, "end", t), self.bank(u, 1, "end", t))
        dve.wait_ge(self.taken, self.x_new_total)
        self.pr.batch_stats(dve, self.next, BATCH - 1)

    def split(self, act, p, slot):
        act.wait_ge(self.w_in, p * 16 + 16)
        self.nc.scalar.copy(self.pr.r_wh[:, slot, :], self.pr.r_raw[:]).then_inc(self.w_hi, 1)

    def swap_halves(self, act, r, w, bank):
        pr, half = self.pr, P // 2
        act.wait_ge(self.work, w + 1)
        after(act, self.turned, r)
        self.nc.scalar.copy(pr.r_sw[0:half, :], pr.ps[half:P, bank, :])
        self.nc.scalar.copy(pr.r_sw[half:P, :], pr.ps[0:half, bank, :]).then_inc(self.swap, 1)

    def turned_hi(self, act, r, part):
        act.wait_ge(self.turned, r + 1)
        self.nc.scalar.copy(part, self.pr.r_t[:]).then_inc(self.t_hi, 1)

    def hi_vt(self, act, w, bank):
        pr = self.pr
        act.wait_ge(self.work, w + 1)
        self.nc.scalar.copy(pr.r_vh[:], pr.ps[:, bank, :].rearrange("p (k d) -> p k d", k=TB)
                            ).then_inc(self.v_hi, 1)

    def hi_out(self, act, n, j):
        act.wait_ge(self.out, n + 1)
        self.nc.scalar.copy(self.pr.r_oth[:, j, :], self.pr.ps[:, OBANK, :]).then_inc(self.o_hi, 1)

    SPLITS = {0: 6, 1: 7, 2: 8, 3: 9, 9: 10, 11: 11, 12: 12, 13: 13, 14: 14, 15: 15}

    def group_scalar(self, act, g, first=False, last=False):
        pr = self.pr
        for b in range(BATCH):
            u, par = g * BATCH + b, b % 2
            u_first, u_last = first and b == 0, last and b == BATCH - 1
            for j in range(R1):
                n = u * R1 + j
                self.probs_hi(act, n, j)
                if j == 2 and not u_last:
                    self.turned_hi(act, self.rotation(u, "k"), pr.r_kh[:, 1 - par, :])
                more = not (u_last and j >= 2)
                if more:
                    r = self.rotation(u, f"q{j}")
                    self.swap_halves(act, r, self.item(u, f"q{j}"), self.bank(u, par, f"q{j}"))
                if not (u_last and j == R1 - 1):
                    self.exponentials(act, n + 1)
                if more:
                    self.turned_hi(act, r, pr.r_qh[:, j % 2, :])
                if j == 0 and not u_first:
                    act.wait_ge(self.work, self.item(u, "y", TB - 1) + 1)
                self.hi_out(act, n, j)
                if j == 1 and not u_last:
                    self.swap_halves(act, self.rotation(u, "k"), self.item(u, "k"), self.bank(u, par, "k"))
                if j == 3 and not u_last:
                    self.hi_vt(act, self.item(u, "vt"), self.bank(u, par, "vt"))
                piece = self.SPLITS.get(R1 * b + j)
                if piece is not None and not (last and piece >= PIECES):
                    self.split(act, g * PIECES + piece, piece % PIECES)

    def scalar(self, act):
        pr = self.pr
        self.split(act, 0, 0)
        pr.norm_scalar(act, self, lambda m: self.split(act, m // TB + 1, m // TB + 1) if m % TB == 1 else None)
        for r, (kind, part) in enumerate((("k", pr.r_kh), ("q0", pr.r_qh), ("q1", pr.r_qh))):
            w = self.AHEAD[kind]
            self.swap_halves(act, r, w, WBANK[w % 2])
            self.turned_hi(act, r, part[:, 1 if kind == "q1" else 0, :])
        self.hi_vt(act, self.AHEAD["vt"], WBANK[self.AHEAD["vt"] % 2])
        self.split(act, 5, 5)
        self.exponentials(act, 0)
        self.group_scalar(act, 0, first=True)
        with act.Fori(1, G1 - 1) as g:
            self.group_scalar(act, g)
        self.group_scalar(act, G1 - 1, last=True)

    def split_lo(self, pool, p, slot):
        pr = self.pr
        pool.wait_ge(self.w_hi, p + 1)
        self.nc.gpsimd.tensor_tensor(pr.r_wl[:, slot, :], pr.r_raw[:], pr.r_wh[:, slot, :].bitcast(F32),
                                     ALU.subtract).then_inc(self.w_lo, 1)

    def rotated(self, pool, r, hi, lo):
        pr = self.pr
        pool.wait_ge(self.sine, r + 1)
        self.nc.gpsimd.tensor_tensor(pr.r_t[:], pr.r_t[:], pr.r_sw[:], ALU.add).then_inc(self.turned, 1)
        pool.wait_ge(self.t_hi, r + 1)
        self.nc.gpsimd.tensor_tensor(lo, pr.r_t[:], hi.bitcast(F32), ALU.subtract).then_inc(self.t_lo, 1)

    def group_gpsimd(self, pool, g, last=False):
        pr = self.pr
        for b in range(BATCH):
            u, par = g * BATCH + b, b % 2
            u_last = last and b == BATCH - 1
            for j in range(R1):
                if not (u_last and j >= 2):
                    self.rotated(pool, self.rotation(u, f"q{j}"), pr.r_qh[:, j % 2, :], pr.r_ql[:, j % 2, :])
                if j == 1 and not u_last:
                    self.rotated(pool, self.rotation(u, "k"), pr.r_kh[:, 1 - par, :], pr.r_kl[:, 1 - par, :])
                piece = self.SPLITS.get(R1 * b + j)
                if piece is not None and not (last and piece >= PIECES):
                    self.split_lo(pool, g * PIECES + piece, piece % PIECES)

    def gpsimd(self, pool):
        pr = self.pr
        for piece in range(5):
            self.split_lo(pool, piece, piece)
        self.clear(pool, [])
        assert self.cleared == self.n_zero
        self.rotated(pool, 0, pr.r_kh[:, 0, :], pr.r_kl[:, 0, :])
        for r, s in ((1, 0), (2, 1)):
            self.rotated(pool, r, pr.r_qh[:, s, :], pr.r_ql[:, s, :])
        self.split_lo(pool, 5, 5)
        self.group_gpsimd(pool, 0)
        with pool.Fori(1, G1 - 1) as g:
            self.group_gpsimd(pool, g)
        self.group_gpsimd(pool, G1 - 1, last=True)

    def load_piece(self, sp, p, rows):
        pr = self.pr
        after(sp, self.w_lo, p)
        sp.dma_start(pr.r_raw[:], pr.io["at1_w"][ds(rows, P), :]).then_inc(self.w_in, 16)

    def sync(self, sp):
        pr = self.pr
        if self.prev is not None:
            sp.wait_ge(self.prev.x_new, self.prev.x_new_total)
        self.load_piece(sp, 0, 0)
        sp.dma_start(pr.r_cos[:], pr.io["at1_cos"]).then_inc(self.tables_in, 16)
        sp.dma_start(pr.r_sin[:], pr.io["at1_sin"]).then_inc(self.tables_in, 16)
        for p in range(1, 6 + PIECES):
            self.load_piece(sp, p, p * P)
        with sp.Fori(1, G1 - 1) as g:
            for k in range(6, 6 + PIECES):
                self.load_piece(sp, g * PIECES + k, g * (PIECES * P) + k * P)
        for k in range(6, PIECES):
            p = (G1 - 1) * PIECES + k
            self.load_piece(sp, p, p * P)


def rope_tables():
    inv = 1.0 / 500000.0 ** (np.arange(0, HD1, 2, dtype=np.float64) / HD1)
    wavelen = 2.0 * np.pi / inv
    low_wl, high_wl = 1024 / 1.0, 1024 / 4.0
    smooth = (1024 / wavelen - 1.0) / (4.0 - 1.0)
    scaled = np.where(wavelen > low_wl, inv / 8.0, inv)
    mid = (wavelen <= low_wl) & (wavelen >= high_wl)
    scaled = np.where(mid, (1 - smooth) * inv / 8.0 + smooth * inv, scaled).astype(np.float32)
    freqs = np.arange(SEQ, dtype=np.float32)[:, None] * scaled[None, :]
    emb = np.concatenate([freqs, freqs], axis=-1)
    return np.cos(emb).T, np.sin(emb).T


def build(nc, io):
    Program(nc, io)


def kernel(**inputs):
    import concourse.bacc as bacc
    from concourse.bass_utils import run_bass_kernel_spmd

    a = {k: np.asarray(v) for k, v in inputs.items()}
    arrays = layout(a)
    nc = bacc.Bacc("TRN2", target_bir_lowering=False, num_devices=1)
    io = {k: nc.dram_tensor(f"in_{k}", v.shape, mybir.dt.from_np(v.dtype), kind="ExternalInput").ap()
          for k, v in arrays.items()}
    io["out"] = nc.dram_tensor("out", (TOK, D), F32, kind="ExternalOutput").ap()
    build(nc, io)
    r = run_bass_kernel_spmd(nc, [{f"in_{k}": v for k, v in arrays.items()}], core_ids=[0])
    return r.results[0]["out"].reshape(BATCH, SEQ, D)


def layout(a):
    def rows(w):
        return w.reshape(P, C, -1)

    out = {"x": a["L0_attn_x"].reshape(TOK, D)}
    gate, up = rows(a["L0_ffn_w_gate"].T), rows(a["L0_ffn_w_up"].T)
    down = a["L0_ffn_w_down"].T
    n = (IT - 1) * P
    gu = np.concatenate([w[:, :, :n].reshape(P, C, IT - 1, P).transpose(2, 0, 1, 3) for w in (gate, up)], 2)
    b = np.stack([a["L0_ffn_b_gate"], a["L0_ffn_b_up"]], 1)
    out["ffn_w"] = np.concatenate([gu.reshape(IT - 1, P, 2 * C * P), down[:n].reshape(IT - 1, P, D),
                                   b[:n].reshape(IT - 1, P, 2)], 2)
    out["ffn_gu_last"] = np.concatenate([gate[:, :, n:], up[:, :, n:]], 1)
    out["ffn_d_last"] = np.concatenate([down[n:], b[n:]], 1)
    out["ffn_bd"] = a["L0_ffn_b_down"]
    out["deq_q"] = a["L1_ffn_qweight"].T.reshape(P, 3, D)
    out["deq_zp"] = a["L1_ffn_weight_zero_point"].reshape(D)
    out["deq_sc"] = a["L1_ffn_weight_scale"].reshape(D)
    out["deq_b"] = a["L1_ffn_bias"]
    q, k, v = (rows(a[f"L0_attn_w{n}"]).reshape(P, C, C, -1).transpose(2, 0, 1, 3) for n in "qkv")
    out["at0_qkv"] = np.concatenate([v, k, q], 3).reshape(C * P, QKV0_W)
    out["at0_o"] = a["L0_attn_wo"]
    q, k, v = (a[f"L1_attn_w{n}"].reshape(P, C, -1, HD1).transpose(2, 0, 1, 3).reshape(-1, P, C * HD1) for n in "qkv")
    o = a["L1_attn_wo"].reshape(G1, R1, P, D)
    q = q.reshape(G1, R1, P, C * HD1)
    out["at1_w"] = np.concatenate([k[:, None], v[:, None], q, o], 1).reshape(G1 * PIECES * P, C * HD1)
    cos, sin = (t.astype(np.float64) * HD1 ** -0.25 for t in rope_tables())
    sin[:HD1 // 2] *= -1
    out["at1_cos"], out["at1_sin"] = cos.astype(np.float32), sin.astype(np.float32)
    return {k: np.ascontiguousarray(v) for k, v in out.items()}
```
